# Optimizing a Trainium2 kernel written in Bass

```python
import numpy as np
import jax
import jax.numpy as jnp

def _softmax(x, axis=-1):
    return jax.nn.softmax(x, axis=axis)
def _gelu(x):
    return jax.nn.gelu(x, approximate=True)
def _silu(x):
    return jax.nn.silu(x)
def _sigmoid(x):
    return jax.nn.sigmoid(x)
def _layernorm(x, axis=-1, eps=1e-5):
    m = jnp.mean(x, axis=axis, keepdims=True)
    v = jnp.var(x, axis=axis, keepdims=True)
    return (x - m) / jnp.sqrt(v + eps)
def _scatter_add(tgt, idx, src, axis=0):
    return tgt.at[idx].add(src)
def _segment_sum(src, seg, n):
    return jax.ops.segment_sum(src, seg, n)

kernel_name = 'mk_conv_seq_d1_conv_nchw512_ab5a8a'

def setup_inputs(seed: int = 0):
    np.random.seed(seed)
    _w = jnp.asarray
    def _rec_inputs():
        import jax
        import jax.numpy as jnp
        _gk = jax.random.key(seed)
        x = -0.0001905 + 0.9999 * jax.random.normal(jax.random.fold_in(_gk, 1), (8, 512, 52, 52), jnp.float32)
        return x
    x = _rec_inputs()
    def _L0_conv_setup():
        import jax, jax.numpy as jnp
        import numpy as np
        from jax import lax
        EPS = 1e-05
        SLOPE = 0.1

        def _bilinear(img, y, x):
            N, C, H, W = img.shape
            y0f = jnp.floor(y)
            x0f = jnp.floor(x)
            wy1 = y - y0f
            wx1 = x - x0f
            wy0 = 1.0 - wy1
            wx0 = 1.0 - wx1
            y0 = y0f.astype(jnp.int32)
            x0 = x0f.astype(jnp.int32)

            def gather(yi, xi):
                valid = ((yi >= 0) & (yi < H) & (xi >= 0) & (xi < W)).astype(img.dtype)
                yc = jnp.clip(yi, 0, H - 1)
                xc = jnp.clip(xi, 0, W - 1)
                g = jax.vmap(lambda im, yy, xx: im[:, yy, xx])(img, yc, xc)
                return g * valid[:, None]
            return gather(y0, x0) * (wy0 * wx0)[:, None] + gather(y0, x0 + 1) * (wy0 * wx1)[:, None] + gather(y0 + 1, x0) * (wy1 * wx0)[:, None] + gather(y0 + 1, x0 + 1) * (wy1 * wx1)[:, None]

        def _dcnv2(x, w_off, b_off, w, b, k, pad):
            N, C, H, W = x.shape
            P = k * k
            om = lax.conv_general_dilated(x, w_off, (1, 1), [(pad, pad), (pad, pad)])
            om = om + b_off[None, :, None, None]
            oy, ox = (om[:, :P], om[:, P:2 * P])
            mask = jax.nn.sigmoid(om[:, 2 * P:])
            ki, kj = jnp.meshgrid(jnp.arange(k), jnp.arange(k), indexing='ij')
            base_y = (jnp.arange(H)[None, :, None] + (ki.reshape(P) - pad)[:, None, None]).astype(x.dtype)
            base_x = (jnp.arange(W)[None, None, :] + (kj.reshape(P) - pad)[:, None, None]).astype(x.dtype)
            sy = oy + base_y[None]
            sx = ox + base_x[None]
            val = _bilinear(x, sy, sx) * mask[:, None]
            out = jnp.einsum('ncphw,ocp->nohw', val, w.reshape(w.shape[0], C, P))
            return out + b[None, :, None, None]

        def _bn_lrelu(x, g, b, m, v):
            s = (g / jnp.sqrt(v + EPS))[None, :, None, None]
            y = (x - m[None, :, None, None]) * s + b[None, :, None, None]
            return jnp.where(y > 0, y, SLOPE * y)
        key = jax.random.key(seed)
        ks = jax.random.split(key, 16)
        N, C, H, W = (8, 512, 52, 52)
        Ch = C // 2
        f = jnp.float32
        x = jax.random.normal(ks[0], (N, C, H, W), f)
        w_off1 = jax.random.normal(ks[1], (3, C, 1, 1), f) * 0.01
        b_off1 = jnp.zeros((3,), f)
        w1 = jax.random.normal(ks[2], (Ch, C, 1, 1), f) * (1.0 / np.sqrt(C))
        b1 = jax.random.normal(ks[3], (Ch,), f) * 0.01
        g1 = 1.0 + 0.1 * jax.random.normal(ks[4], (Ch,), f)
        bb1 = 0.1 * jax.random.normal(ks[5], (Ch,), f)
        m1 = 0.1 * jax.random.normal(ks[6], (Ch,), f)
        v1 = 0.5 + jax.random.uniform(ks[7], (Ch,), f)
        w_off2 = jax.random.normal(ks[8], (27, Ch, 3, 3), f) * 0.01
        b_off2 = jnp.zeros((27,), f)
        w2 = jax.random.normal(ks[9], (C, Ch, 3, 3), f) * (1.0 / np.sqrt(Ch * 9))
        b2 = jax.random.normal(ks[10], (C,), f) * 0.01
        g2 = 1.0 + 0.1 * jax.random.normal(ks[11], (C,), f)
        bb2 = 0.1 * jax.random.normal(ks[12], (C,), f)
        m2 = 0.1 * jax.random.normal(ks[13], (C,), f)
        v2 = 0.5 + jax.random.uniform(ks[14], (C,), f)
        return dict(x=x, w_off1=w_off1, b_off1=b_off1, w1=w1, b1=b1, g1=g1, bb1=bb1, m1=m1, v1=v1, w_off2=w_off2, b_off2=b_off2, w2=w2, b2=b2, g2=g2, bb2=bb2, m2=m2, v2=v2)
    _L0_conv_all = _L0_conv_setup()
    _L0_conv_in = {k: v for k, v in _L0_conv_all.items() if k in ('w_off1', 'b_off1', 'w1', 'b1', 'g1', 'bb1', 'm1', 'v1', 'w_off2', 'b_off2', 'w2', 'b2', 'g2', 'bb2', 'm2', 'v2', )}
    del _L0_conv_all

    return {
        "x": x,
        "L0_conv_w_off1": _L0_conv_in["w_off1"],
        "L0_conv_b_off1": _L0_conv_in["b_off1"],
        "L0_conv_w1": _L0_conv_in["w1"],
        "L0_conv_b1": _L0_conv_in["b1"],
        "L0_conv_g1": _L0_conv_in["g1"],
        "L0_conv_bb1": _L0_conv_in["bb1"],
        "L0_conv_m1": _L0_conv_in["m1"],
        "L0_conv_v1": _L0_conv_in["v1"],
        "L0_conv_w_off2": _L0_conv_in["w_off2"],
        "L0_conv_b_off2": _L0_conv_in["b_off2"],
        "L0_conv_w2": _L0_conv_in["w2"],
        "L0_conv_b2": _L0_conv_in["b2"],
        "L0_conv_g2": _L0_conv_in["g2"],
        "L0_conv_bb2": _L0_conv_in["bb2"],
        "L0_conv_m2": _L0_conv_in["m2"],
        "L0_conv_v2": _L0_conv_in["v2"],
    }

def reference(x, L0_conv_w_off1, L0_conv_b_off1, L0_conv_w1, L0_conv_b1, L0_conv_g1, L0_conv_bb1, L0_conv_m1, L0_conv_v1, L0_conv_w_off2, L0_conv_b_off2, L0_conv_w2, L0_conv_b2, L0_conv_g2, L0_conv_bb2, L0_conv_m2, L0_conv_v2):
    import jax
    import jax.numpy as jnp
    def _L0_conv_ref(x, w_off1, b_off1, w1, b1, g1, bb1, m1, v1, w_off2, b_off2, w2, b2, g2, bb2, m2, v2):
        import jax, jax.numpy as jnp
        import numpy as np
        from jax import lax
        EPS = 1e-05
        SLOPE = 0.1

        def _bilinear(img, y, x):
            N, C, H, W = img.shape
            y0f = jnp.floor(y)
            x0f = jnp.floor(x)
            wy1 = y - y0f
            wx1 = x - x0f
            wy0 = 1.0 - wy1
            wx0 = 1.0 - wx1
            y0 = y0f.astype(jnp.int32)
            x0 = x0f.astype(jnp.int32)

            def gather(yi, xi):
                valid = ((yi >= 0) & (yi < H) & (xi >= 0) & (xi < W)).astype(img.dtype)
                yc = jnp.clip(yi, 0, H - 1)
                xc = jnp.clip(xi, 0, W - 1)
                g = jax.vmap(lambda im, yy, xx: im[:, yy, xx])(img, yc, xc)
                return g * valid[:, None]
            return gather(y0, x0) * (wy0 * wx0)[:, None] + gather(y0, x0 + 1) * (wy0 * wx1)[:, None] + gather(y0 + 1, x0) * (wy1 * wx0)[:, None] + gather(y0 + 1, x0 + 1) * (wy1 * wx1)[:, None]

        def _dcnv2(x, w_off, b_off, w, b, k, pad):
            N, C, H, W = x.shape
            P = k * k
            om = lax.conv_general_dilated(x, w_off, (1, 1), [(pad, pad), (pad, pad)])
            om = om + b_off[None, :, None, None]
            oy, ox = (om[:, :P], om[:, P:2 * P])
            mask = jax.nn.sigmoid(om[:, 2 * P:])
            ki, kj = jnp.meshgrid(jnp.arange(k), jnp.arange(k), indexing='ij')
            base_y = (jnp.arange(H)[None, :, None] + (ki.reshape(P) - pad)[:, None, None]).astype(x.dtype)
            base_x = (jnp.arange(W)[None, None, :] + (kj.reshape(P) - pad)[:, None, None]).astype(x.dtype)
            sy = oy + base_y[None]
            sx = ox + base_x[None]
            val = _bilinear(x, sy, sx) * mask[:, None]
            out = jnp.einsum('ncphw,ocp->nohw', val, w.reshape(w.shape[0], C, P))
            return out + b[None, :, None, None]

        def _bn_lrelu(x, g, b, m, v):
            s = (g / jnp.sqrt(v + EPS))[None, :, None, None]
            y = (x - m[None, :, None, None]) * s + b[None, :, None, None]
            return jnp.where(y > 0, y, SLOPE * y)
        h = _bn_lrelu(_dcnv2(x, w_off1, b_off1, w1, b1, 1, 0), g1, bb1, m1, v1)
        h = _bn_lrelu(_dcnv2(h, w_off2, b_off2, w2, b2, 3, 1), g2, bb2, m2, v2)
        return x + h

    def _gn(v, G=32, eps=1e-5):
        B_, C_, H_, W_ = v.shape
        g = v.reshape(B_, G, C_ // G, H_, W_)
        m = jnp.mean(g, axis=(2, 3, 4), keepdims=True)
        s = jnp.var(g, axis=(2, 3, 4), keepdims=True)
        return ((g - m) / jnp.sqrt(s + eps)).reshape(v.shape)

    def _ln_c(v, eps=1e-6):
        m = jnp.mean(v, axis=1, keepdims=True)
        s = jnp.var(v, axis=1, keepdims=True)
        return (v - m) / jnp.sqrt(s + eps)

    def _ln_t(v, eps=1e-5):
        m = jnp.mean(v, axis=-1, keepdims=True)
        s = jnp.var(v, axis=-1, keepdims=True)
        return (v - m) / jnp.sqrt(s + eps)

    def _to_tokens(v):
        B_, C_, H_, W_ = v.shape
        return v.reshape(B_, C_, H_ * W_).transpose(0, 2, 1)
    def _from_tokens(t, like):
        B_, C_, H_, W_ = like.shape
        return t.transpose(0, 2, 1).reshape(B_, C_, H_, W_)

    x = _L0_conv_ref(x, L0_conv_w_off1, L0_conv_b_off1, L0_conv_w1, L0_conv_b1, L0_conv_g1, L0_conv_bb1, L0_conv_m1, L0_conv_v1, L0_conv_w_off2, L0_conv_b_off2, L0_conv_w2, L0_conv_b2, L0_conv_g2, L0_conv_bb2, L0_conv_m2, L0_conv_v2)
    return x


_drawn_inputs = setup_inputs


def setup_inputs(seed=0):
    import zlib

    import numpy as np

    out = dict(_drawn_inputs(seed))
    spreads = {'L0_conv_b_off1': (0.0, 0.557), 'L0_conv_b_off2': (0.0, 0.668)}
    factors = {'L0_conv_b1': 8.0,
     'L0_conv_g1': 5.959,
     'L0_conv_v1': 3.916,
     'L0_conv_w_off2': 3.509,
     'L0_conv_b2': 7.004,
     'L0_conv_g2': 4.165,
     'L0_conv_v2': 3.048}
    for name, (base, spread) in spreads.items():
        noise = np.random.default_rng([zlib.crc32(name.encode()), seed]).standard_normal(out[name].shape)
        drawn = base * np.exp(spread * noise) if base else spread * noise
        out[name] = jnp.asarray(drawn.astype(out[name].dtype))
    for name, factor in factors.items():
        out[name] = (out[name] * factor).astype(out[name].dtype)
    return out
```

```python
from contextlib import ExitStack

import numpy as np

import concourse.bass as bass
from concourse import mybir

N_IMAGES, C_OUT, HEIGHT, WIDTH = 8, 512, 52, 52
C_MID = C_OUT // 2
IMAGE = HEIGHT * WIDTH
P = 128
PIXELS = N_IMAGES * IMAGE
TILES = PIXELS // P
CHUNK = 13
CHUNKS = TILES // CHUNK
CHUNK_PX = CHUNK * P
TAPS = 9
GROUP = 3
GROUPS = TAPS // GROUP
TABLE_ROWS = PIXELS + WIDTH
EPS, SLOPE = 1e-5, 0.1
ROUND = 1.5 * 2.0**23
HALVES = ((0, 7), (7, 6))
SLOTS = 7
TAIL = 2 * P


def pixel_constants():
    g = np.arange(PIXELS)
    y, x, first = g % IMAGE // WIDTH, g % WIDTH, g // IMAGE * IMAGE + WIDTH
    where = np.zeros((TILES + 1, P, 3), np.float32)
    where[0, :, 2] = WIDTH
    where[1:] = np.stack([y, x, first], -1).reshape(TILES, P, 3)
    inside = np.zeros((TILES + 1, P, TAPS), np.float32)
    for k in range(TAPS):
        ty, tx = y + k // 3 - 1, x + k % 3 - 1
        inside[1:, :, k] = ((ty >= 0) & (ty < HEIGHT) & (tx >= 0) & (tx < WIDTH)).reshape(TILES, P)
    shift = np.array([[k // 3 - 1 for k in range(TAPS)] + [k % 3 - 1 for k in range(TAPS)]], np.float32)
    return where.transpose(1, 0, 2).copy(), inside.transpose(1, 0, 2).copy(), shift


def pieces(first, count):
    end = (first // IMAGE + 1) * IMAGE
    cut = end - first if first < end < first + count else count // 2
    return [((first + o) // IMAGE, (first + o) % IMAGE, o, n) for o, n in ((0, cut), (cut, count - cut))]


def deformable_kernel(nc, x, w1, norm1, w_off2, w2, norm2, b_off1, b_off2, where, inside, shift,
                      identity, out):
    f32, f32r = mybir.dt.float32, mybir.dt.float32r
    u32, u16 = mybir.dt.uint32, mybir.dt.uint16
    ALU, ACT, AX = mybir.AluOpType, mybir.ActivationFunctionType, mybir.AxisListType
    ds = bass.ds

    table1 = nc.dram_tensor("table1", [TABLE_ROWS, 2 * C_MID], f32, kind="Internal").ap()
    table2 = nc.dram_tensor("table2", [TABLE_ROWS, 2 * C_MID], f32, kind="Internal").ap()
    KT1 = C_OUT // P
    KT2 = C_MID // P
    N1 = C_MID + 3
    N_OFF = 3 * TAPS
    SLABS = TAPS * KT2
    NORMS = 5

    with ExitStack() as ctx:
        def sb(name, shape, dt=f32):
            return ctx.enter_context(nc.sbuf_tensor(name, shape, dt))

        def ps(name, cols):
            return ctx.enter_context(nc.psum_tensor(name, [P, cols], f32))

        def sem(name):
            return ctx.enter_context(nc.semaphore(name))

        w2_hi = sb("w2_hi", [P, SLABS, C_OUT], f32r)
        w2_lo = sb("w2_lo", [P, SLABS, C_OUT], f32r)
        val_hi = sb("val_hi", [P, GROUPS, GROUP * C_MID], f32r)
        val_lo = sb("val_lo", [P, GROUPS, GROUP * C_MID], f32r)
        weights2 = sb("weights2", [P, 4, (TILES + 1) * TAPS])
        index2 = sb("index2", [P, (TILES + 1) * TAPS], u16)
        bias2 = sb("bias2", [P, C_OUT])
        ident = sb("ident", [P, P])
        boff1 = sb("boff1", [P, 3])
        boff2 = sb("boff2", [P, N_OFF])
        shifts = sb("shifts", [P, 2 * TAPS])
        row_cur = sb("row_cur", [P, 16], u32)

        area_a = sb("area_a", [P, KT1 * CHUNK_PX + KT1 * N1])
        x_sb = area_a[:, 0:KT1 * CHUNK_PX].rearrange("p (k n) -> p k n", k=KT1)
        w1_sb = area_a[:, KT1 * CHUNK_PX:].rearrange("p (k n) -> p k n", k=KT1)
        HT = TAIL + CHUNK_PX + 64
        h_stage = area_a[:, 0:CHUNK * C_MID].rearrange("p (t c) -> p t c", t=CHUNK)
        h_t = area_a[:, CHUNK * C_MID:CHUNK * C_MID + KT2 * HT].rearrange("p (k n) -> p k n", k=KT2)
        stage = x_sb
        area_b = sb("area_b", [P, TAPS * 4 * C_MID])
        HALF_SLABS = SLABS // 2
        w2_raw = area_b[:, 0:HALF_SLABS * C_OUT].rearrange("p (s n) -> p s n", s=HALF_SLABS)
        at = HALF_SLABS * C_OUT
        norm1_sb = area_b[:, at:at + NORMS * C_MID].rearrange("p (v n) -> p v n", v=NORMS)
        at += NORMS * C_MID
        norm2_sb = area_b[:, at:at + NORMS * C_OUT].rearrange("p (v n) -> p v n", v=NORMS)
        gather1 = area_b[:, 0:SLOTS * 4 * C_MID].rearrange("p (s q c) -> p s q c", s=SLOTS, q=4)
        at = SLOTS * 4 * C_MID
        inside_sb = area_b[:, at:at + (TILES + 1) * TAPS].rearrange("p (t k) -> p t k", k=TAPS)
        gather2 = area_b[:, :].rearrange("p (s q c) -> p s q c", s=TAPS, q=4)
        y_stage = weights2[:, :, :].rearrange("p q n -> p (q n)")[:, 0:CHUNK * N1]\
            .rearrange("p (t c) -> p t c", t=CHUNK)
        C_SIZE = 4050
        area_c = sb("area_c", [P, C_SIZE])
        at = 0

        def part(n):
            nonlocal at
            at += n
            assert at <= C_SIZE, at
            return area_c[:, at - n:at]

        woff_sb = part(KT2 * TAPS * N_OFF).rearrange("p (k n) -> p k n", k=KT2)
        weights1 = part(4 * TILES).rearrange("p (q t) -> p q t", q=4)
        index1 = part(TILES)
        bias1 = part(C_MID)
        where_sb = part((TILES + 1) * 3).rearrange("p (t v) -> p t v", v=3)
        om = part(CHUNK * N_OFF).rearrange("p (t n) -> p t n", t=CHUNK)
        spot = part(CHUNK * 2 * TAPS)
        corner = part(CHUNK * 2 * TAPS)
        near = part(CHUNK * 2 * TAPS)
        far = part(CHUNK * 2 * TAPS)
        gate = part(CHUNK * TAPS)
        prod = far_y = part(TAPS * N_OFF)
        at = 0
        val = part(TAPS * C_MID).rearrange("p (g k c) -> p g k c", g=GROUPS, k=GROUP)
        acc_sb = part(C_OUT)
        z_sb = part(C_OUT)
        z_act = part(C_OUT)
        h_pre = val_tmp = sb("h_pre", [P, 2, C_MID])

        psum_t = ps("psum_t", GROUPS * 1024)
        psum_acc = ps("psum_acc", 512)
        psum_out = ps("psum_out", 512)

        gather_cleared = sem("gather_cleared")

        def group_t(g):
            return psum_t[:, 1024 * g:1024 * g + GROUP * C_MID]

        def sample_plan(dve, link, gate_ready, om_ready, tiles, k, raw, slot, base, wts, rows,
                        gate_count):
            n = tiles * 2 * k
            o = om[:, 0:tiles, 0:3 * k]

            def two(t):
                return t[:, 0:n].rearrange("p (t v) -> p t v", t=tiles)

            def axis(t, a):
                return two(t)[:, :, a * k:(a + 1) * k]

            b_off = (boff1 if k == 1 else boff2)[:, 0:3 * k]
            yx = where_sb[:, ds(slot, tiles), 0:2]
            first = where_sb[:, ds(slot, tiles), 2:3]
            m = gate[:, 0:tiles * k].rearrange("p (t k) -> p t k", k=k)
            nc.vector.tensor_tensor(o, raw, b_off.unsqueeze(1).to_broadcast([P, tiles, 3 * k]), ALU.add)\
                .then_inc(om_ready, 1)
            dve.wait_ge(om_ready, gate_count + 1)
            if k == 1:
                link(nc.vector.tensor_tensor(two(spot), o[:, :, 0:2], yx, ALU.add))
            else:
                for a in range(2):
                    last = nc.vector.tensor_tensor(
                        axis(spot, a), yx[:, :, a:a + 1].to_broadcast([P, tiles, k]),
                        shifts[:, a * k:(a + 1) * k].unsqueeze(1).to_broadcast([P, tiles, k]), ALU.add)
                link(last)
                link(nc.vector.tensor_tensor(two(spot), o[:, :, 0:2 * k], two(spot), ALU.add))
            link(nc.vector.tensor_scalar(two(corner), two(spot), 0.0, float(HEIGHT - 1), ALU.max, ALU.min))
            link(nc.vector.tensor_scalar(two(corner), two(corner), -0.5, ROUND, ALU.add, ALU.add))
            link(nc.vector.tensor_scalar(two(corner), two(corner), ROUND, None, ALU.subtract))
            link(nc.vector.tensor_tensor(two(spot), two(spot), two(corner), ALU.subtract))
            link(nc.vector.tensor_scalar(two(near), two(spot), -1.0, 1.0, ALU.mult, ALU.add))
            link(nc.vector.scalar_tensor_tensor(out=two(near), in0=two(spot), scalar=1.0, in1=two(near),
                                                op0=ALU.add, op1=ALU.min))
            link(nc.vector.tensor_scalar(two(far), two(spot), -1.0, 2.0, ALU.mult, ALU.add))
            link(nc.vector.scalar_tensor_tensor(out=two(far), in0=two(far), scalar=0.0, in1=two(spot),
                                                op0=ALU.max, op1=ALU.min))
            dve.wait_ge(gate_ready, gate_count)
            for t in (near, far):
                last = nc.vector.scalar_tensor_tensor(out=axis(t, 0), in0=axis(t, 0), scalar=0.0, in1=m,
                                                      op0=ALU.max, op1=ALU.mult)
            link(last)
            for q, (ty, tx) in enumerate(((near, near), (far, near), (near, far), (far, far))):
                nc.vector.scalar_tensor_tensor(
                    out=wts[:, q, base].rearrange("p (t k) -> p t k", k=k), in0=axis(tx, 1), scalar=0.0,
                    in1=axis(ty, 0), op0=ALU.max, op1=ALU.mult)
            link(nc.vector.scalar_tensor_tensor(out=axis(spot, 0), in0=axis(corner, 0), scalar=float(WIDTH),
                                                in1=axis(corner, 1), op0=ALU.mult, op1=ALU.add))
            link(nc.vector.tensor_tensor(rows[:, base].rearrange("p (t k) -> p t k", k=k), axis(spot, 0),
                                         first.to_broadcast([P, tiles, k]), ALU.add))

        def linker(dve, done):
            count = [0]

            def link(ins):
                count[0] += 1
                ins.then_inc(done, 1)
                dve.wait_ge(done, count[0])
            return link, count

        def table_writes(eng, table, source, c, half, written):
            j, n = HALVES[half]
            for row, col in ((WIDTH, 0), (0, C_MID)):
                dst = table[ds(c * CHUNK_PX + row + j * P, n * P), col:col + C_MID]
                eng.dma_start(dst.rearrange("(t p) c -> p t c", p=P), source[:, j:j + n, 0:C_MID])\
                    .then_inc(written, 16)

        with ExitStack() as phase:
            def sem(name):
                return phase.enter_context(nc.semaphore(name))

            const_loaded = sem("const_loaded")
            x_loaded = [sem("x_loaded_a"), sem("x_loaded_b")]
            raw_loaded = [sem("raw_loaded_a"), sem("raw_loaded_b")]
            x_used = sem("x_used")
            y_copied = sem("y_copied")
            table_written = [sem("table_written_a"), sem("table_written_b")]
            root_ready = sem("root_ready")
            var_ready = sem("var_ready")
            edge_cleared = sem("edge_cleared")
            edge_written = sem("edge_written")
            w1_scaled = sem("w1_scaled")
            w2_split = sem("w2_split")
            om_ready = sem("om_ready")
            gate_ready = sem("gate_ready")
            chain = sem("chain")
            setup = sem("setup")
            block = phase.enter_context(nc.Block())
            CONSTS = 10

            def y_bank(j):
                b = j % 7
                return psum_acc[:, 0:N1] if b == 6 else psum_t[:, 512 * b:512 * b + N1]

            @block.sync
            def _(sp):
                sp.dma_start(w1_sb, w1.rearrange("(k p) n -> p k n", p=P)).then_inc(const_loaded, 16)
                sp.dma_start(norm1_sb, norm1.unsqueeze(0).to_broadcast([P, NORMS, C_MID]))\
                    .then_inc(const_loaded, 16)
                for c in range(CHUNKS):
                    for half, (j, n) in enumerate(HALVES):
                        if c:
                            sp.wait_ge(x_used, CHUNK * (c - 1) + j + n)
                        for image, px, o, count in pieces(c * CHUNK_PX + j * P, n * P):
                            sp.dma_start(x_sb[:, :, j * P + o:j * P + o + count],
                                         x[image].rearrange("(k p) n -> p k n", p=P)[:, :, px:px + count])\
                                .then_inc(x_loaded[half], 16)
                    if c == 0:
                        for dst, src in (
                            (norm2_sb, norm2.unsqueeze(0).to_broadcast([P, NORMS, C_OUT])),
                            (boff1[:, :], b_off1.to_broadcast([P, 3])),
                            (boff2[:, :], b_off2.to_broadcast([P, N_OFF])),
                            (shifts[:, :], shift.to_broadcast([P, 2 * TAPS])),
                            (ident[:, :], identity),
                            (where_sb, where),
                        ):
                            sp.dma_start(dst, src).then_inc(const_loaded, 16)
                        for k in range(KT2):
                            sp.dma_start(woff_sb[:, k, :].rearrange("p (t n) -> p t n", t=TAPS),
                                         w_off2[:, k * P:(k + 1) * P, :].rearrange("t p n -> p t n"))\
                                .then_inc(const_loaded, 16)

            @block.gpsimd
            def _(pool):
                nc.gpsimd.memset(h_pre[:, 0, :], 0.0).then_inc(edge_cleared, 1)
                pool.wait_ge(edge_cleared, 1)
                for table in (table1, table2):
                    for row, col in ((0, 0), (PIXELS, C_MID)):
                        pool.dma_start(table[row:row + WIDTH, col:col + C_MID], h_pre[0:WIDTH, 0, :])\
                            .then_inc(edge_written, 16)
                for part_no in range(2):
                    if part_no:
                        pool.wait_ge(w2_split, HALF_SLABS)
                    pool.dma_start(w2_raw, w2[part_no * HALF_SLABS * P:(part_no + 1) * HALF_SLABS * P, :]
                                   .rearrange("(s p) n -> p s n", p=P)).then_inc(raw_loaded[part_no], 16)
                pool.wait_ge(edge_written, 64)

            @block.tensor
            def _(pe):
                pe.wait_ge(w1_scaled, 1)
                with pe.Fori(0, CHUNKS) as c:
                    for half, (j0, n) in enumerate(HALVES):
                        pe.wait_ge(x_loaded[half], (c + 1) * 32)
                        for j in range(j0, j0 + n):
                            pe.wait_ge(y_copied, c * CHUNK + j + 1)
                            for k in range(KT1):
                                last = nc.tensor.matmul(y_bank(j),
                                                        x_sb[:, k, j * P:(j + 1) * P], w1_sb[:, k, :],
                                                        start=(k == 0), stop=(k == KT1 - 1))
                            last.then_inc(x_used, 1)

            @block.scalar
            def _(act):
                for layer, norm in ((0, norm1_sb), (1, norm2_sb)):
                    act.wait_ge(var_ready, layer + 1)
                    nc.scalar.activation(norm[:, 1, :], norm[:, 1, :], ACT.Sqrt).then_inc(root_ready, 1)
                act.sem_inc(y_copied, 6)
                for half in range(2):
                    act.sem_inc(table_written[half], 32)
                with act.Fori(0, CHUNKS) as c:
                    for half, (j0, n) in enumerate(HALVES):
                        act.wait_ge(table_written[half], (c + 1) * 32)
                        act.wait_ge(om_ready, c + 1)
                        for j in range(j0, j0 + n):
                            act.wait_ge(x_used, c * CHUNK + j + 1)
                            nc.scalar.activation(y_stage[:, j, :], y_bank(j), ACT.Copy).then_inc(y_copied, 1)
                        act.wait_ge(y_copied, c * CHUNK + 6 + j0 + n)
                        table_writes(act, table1, y_stage, c, half, table_written[half])
                    act.wait_ge(om_ready, c + 2)
                    nc.scalar.activation(gate[:, 0:CHUNK].unsqueeze(2), om[:, :, 2:3], ACT.Sigmoid)\
                        .then_inc(gate_ready, 1)
                for half in range(2):
                    act.wait_ge(table_written[half], (CHUNKS + 1) * 32)

            @block.vector
            def _(dve):
                link, count = linker(dve, setup)

                def fold(norm, bias):
                    link(nc.vector.reciprocal(norm[:, 1, :], norm[:, 1, :]))
                    link(nc.vector.tensor_tensor(norm[:, 0, :], norm[:, 0, :], norm[:, 1, :], ALU.mult))
                    link(nc.vector.tensor_tensor(bias, norm[:, 4, :], norm[:, 2, :], ALU.subtract))
                    link(nc.vector.tensor_tensor(bias, bias, norm[:, 0, :], ALU.mult))
                    link(nc.vector.tensor_tensor(bias, bias, norm[:, 3, :], ALU.add))

                dve.sem_inc(om_ready, 1)
                dve.wait_ge(const_loaded, 16 * CONSTS)
                for norm in (norm1_sb, norm2_sb):
                    nc.vector.tensor_scalar(norm[:, 1, :], norm[:, 1, :], EPS, None, ALU.add)\
                        .then_inc(var_ready, 1)
                dve.wait_ge(root_ready, 1)
                fold(norm1_sb, bias1)
                for k in range(KT1):
                    last = nc.vector.tensor_tensor(w1_sb[:, k, 0:C_MID], w1_sb[:, k, 0:C_MID],
                                                   norm1_sb[:, 0, :], ALU.mult)
                last.then_inc(w1_scaled, 1)
                dve.wait_ge(root_ready, 2)
                fold(norm2_sb, bias2[:, :])

                def split(part_no):
                    dve.wait_ge(raw_loaded[part_no], 16)
                    for s in range(HALF_SLABS):
                        hi = w2_hi[:, part_no * HALF_SLABS + s, :]
                        lo = w2_lo[:, part_no * HALF_SLABS + s, :]
                        link(nc.vector.tensor_tensor(w2_raw[:, s, :], w2_raw[:, s, :], norm2_sb[:, 0, :],
                                                     ALU.mult))
                        link(nc.vector.tensor_copy(hi, w2_raw[:, s, :]))
                        nc.vector.tensor_tensor(lo, w2_raw[:, s, :], hi.bitcast(f32), ALU.subtract)\
                            .then_inc(w2_split, 1)

                def plan_chunk(c):
                    dve.wait_ge(y_copied, (c + 1) * CHUNK + 6)
                    steps = [0]

                    def link_in_chunk(ins):
                        steps[0] += 1
                        ins.then_inc(chain, 1)
                        dve.wait_ge(chain, c * PLAN_STEPS_1 + steps[0])

                    sample_plan(dve, link_in_chunk, gate_ready, om_ready, CHUNK, 1,
                                y_stage[:, :, C_MID:], c * CHUNK + 1, ds(c * CHUNK, CHUNK), weights1,
                                index1, c + 1)
                    assert steps[0] == PLAN_STEPS_1, steps

                split(0)
                plan_chunk(0)
                split(1)
                with dve.Fori(1, CHUNKS) as c:
                    plan_chunk(c)

        with ExitStack() as phase:
            def sem(name):
                return phase.enter_context(nc.semaphore(name))

            inside_loaded = sem("inside_loaded")
            h_t_cleared = sem("h_t_cleared")
            rows_copied = sem("rows_copied")
            gathered = [sem(f"gathered1_{s}") for s in range(SLOTS)]
            sampled = sem("sampled")
            summed = sem("summed")
            h_ready = sem("h_ready")
            h_transposed = sem("h_transposed")
            h_t_ready = sem("h_t_ready")
            tail_kept = sem("tail_kept")
            convolved = sem("convolved")
            masked = sem("masked")
            reduced = sem("reduced")
            table_written = [sem("table2_written_a"), sem("table2_written_b")]
            om_ready = sem("om2_ready")
            gate_ready = sem("gate2_ready")
            chain = sem("chain2")
            block = phase.enter_context(nc.Block())

            def bank(j):
                j %= CHUNK
                return 512 * (j % 3 if j < CHUNK - 2 else j - (CHUNK - 2))

            def t_bank(j):
                return psum_t[:, bank(j):bank(j) + C_MID]

            def off_bank(j):
                return psum_t[:, 3 * 512 + bank(j):3 * 512 + bank(j) + TAPS * N_OFF]

            @block.sync
            def _(sp):
                sp.dma_start(inside_sb, inside).then_inc(inside_loaded, 16)
                sp.wait_ge(inside_loaded, 16)

            @block.gpsimd
            def _(pool):
                with pool.Fori(0, CHUNKS) as c:
                    for half, (j0, n) in enumerate(HALVES):
                        pool.wait_ge(sampled, c * CHUNK + j0 + n)
                        nc.gpsimd.tensor_copy(row_cur[:, j0:j0 + n], index1[:, ds(c * CHUNK + j0, n)])\
                            .then_inc(rows_copied, 1)
                        pool.wait_ge(rows_copied, 2 * c + half + 1)
                        for j in range(j0, j0 + n):
                            back = SLOTS if j >= SLOTS else CHUNK if j + SLOTS >= CHUNK else CHUNK - SLOTS
                            pool.wait_ge(sampled, c * CHUNK + j + 1 - back + CHUNK)
                            pool.sem_inc(gather_cleared, 1)
                            nc.gpsimd.indirect_dma_start(
                                gather1[:, j % SLOTS, :, :].rearrange("p q c -> p (q c)"), None,
                                table1, bass.IndirectOffsetOnAxis(ap=row_cur[:, j:j + 1], axis=0))\
                                .then_inc(gathered[j % SLOTS], 16)

            def conv_offsets(j):
                at = TAIL + (j - 1) * P
                for k in range(TAPS):
                    s = at + (k // 3 - 1) * WIDTH + k % 3 - 1
                    for kt in range(KT2):
                        last = nc.tensor.matmul(off_bank(j)[:, k * N_OFF:(k + 1) * N_OFF],
                                                h_t[:, kt, s:s + P],
                                                woff_sb[:, kt, k * N_OFF:(k + 1) * N_OFF],
                                                start=(kt == 0), stop=(kt == KT2 - 1))
                last.then_inc(convolved, 1)

            @block.tensor
            def _(pe):
                def transpose_h(c, j):
                    pe.wait_ge(h_ready, c * CHUNK + j + 1)
                    pe.wait_ge(h_t_ready, c * CHUNK + j + 1)
                    for kt in range(KT2):
                        last = nc.tensor.transpose(t_bank(j)[:, kt * P:(kt + 1) * P],
                                                   h_stage[:, j, kt * P:(kt + 1) * P], ident[:, :])
                    last.then_inc(h_transposed, 1)

                with pe.Fori(0, CHUNKS) as c:
                    for j in range(CHUNK):
                        transpose_h(c, j)
                        pe.wait_ge(h_t_ready, c * CHUNK + j + 1 + 2)
                        if j == 0:
                            pe.wait_ge(tail_kept, c + 1)
                        pe.wait_ge(masked, c * CHUNK + j + 1)
                        conv_offsets(j)
                pe.wait_ge(masked, CHUNKS * CHUNK + 1)
                conv_offsets(CHUNK)

            @block.scalar
            def _(act):
                act.sem_inc(h_t_ready, 2)
                for half in range(2):
                    act.sem_inc(table_written[half], 32)
                act.wait_ge(h_t_cleared, 1)
                act.sem_inc(tail_kept, 1)
                with act.Fori(0, CHUNKS) as c:
                    for half, (j0, n) in enumerate(HALVES):
                        for j in range(j0, j0 + n):
                            act.wait_ge(h_transposed, c * CHUNK + j + 1)
                            act.wait_ge(convolved, c * CHUNK + j)
                            nc.scalar.activation(h_t[:, :, TAIL + j * P:TAIL + (j + 1) * P],
                                                 t_bank(j).rearrange("p (k n) -> p k n", k=KT2),
                                                 ACT.Copy).then_inc(h_t_ready, 1)
                        act.wait_ge(h_ready, c * CHUNK + j0 + n)
                        table_writes(act, table2, h_stage, c, half, table_written[half])
                    act.wait_ge(h_t_ready, (c + 1) * CHUNK + 2)
                    nc.scalar.activation(h_t[:, :, 0:TAIL], h_t[:, :, CHUNK_PX:CHUNK_PX + TAIL],
                                         ACT.Copy).then_inc(tail_kept, 1)
                    act.wait_ge(tail_kept, c + 2)
                    act.wait_ge(om_ready, c + 2)
                    nc.scalar.activation(gate.rearrange("p (t k) -> p t k", k=TAPS),
                                         om[:, :, 2 * TAPS:], ACT.Sigmoid).then_inc(gate_ready, 1)
                act.wait_ge(om_ready, CHUNKS + 2)
                act.wait_ge(gate_ready, CHUNKS)
                nc.scalar.activation(gate[:, 0:TAPS].unsqueeze(1), om[:, 0:1, 2 * TAPS:],
                                     ACT.Sigmoid).then_inc(gate_ready, 1)
                for half in range(2):
                    act.wait_ge(table_written[half], (CHUNKS + 1) * 32)

            @block.vector
            def _(dve):
                nc.vector.memset(h_t, 0.0).then_inc(h_t_cleared, 1)
                dve.sem_inc(sampled, CHUNK)
                dve.sem_inc(masked, 2)
                dve.sem_inc(om_ready, 1)
                dve.wait_ge(inside_loaded, 16)

                def sample_h(c, j):
                    nth = c * CHUNK + j
                    uses = 2 if j + SLOTS < CHUNK or j >= SLOTS else 1
                    nth_use = c * uses + (1 if j >= SLOTS else 0)
                    dve.wait_ge(gathered[j % SLOTS], (nth_use + 1) * 16)
                    v = h_pre[:, j % 2, :]
                    for q in range(4):
                        ins = nc.vector.scalar_tensor_tensor(
                            out=v, in0=gather1[:, j % SLOTS, q, :], scalar=weights1[:, q, ds(nth, 1)],
                            in1=bias1 if q == 0 else v, op0=ALU.mult, op1=ALU.add)
                        if q < 3:
                            ins.then_inc(summed, 1)
                            dve.wait_ge(summed, 3 * nth + q + 1)
                    ins.then_inc(sampled, 1)
                    dve.wait_ge(sampled, nth + 1 + CHUNK)
                    nc.vector.scalar_tensor_tensor(out=h_stage[:, j, :], in0=v, scalar=SLOPE, in1=v,
                                                   op0=ALU.mult, op1=ALU.max).then_inc(h_ready, 1)

                def offsets(c, j):
                    nth = c * CHUNK + j
                    dve.wait_ge(convolved, nth + 1)
                    dve.wait_ge(reduced, nth + 1)
                    taps = prod.rearrange("p (k n) -> p k n", k=TAPS)
                    nc.vector.tensor_tensor(
                        taps, off_bank(j).rearrange("p (k n) -> p k n", k=TAPS),
                        inside_sb[:, ds(nth, 1), :].rearrange("p t k -> p (t k)").unsqueeze(2)
                        .to_broadcast([P, TAPS, N_OFF]), ALU.mult).then_inc(masked, 1)
                    dve.wait_ge(masked, nth + 1 + 2)
                    nc.vector.tensor_reduce(om[:, j % CHUNK, :], prod.rearrange("p (k n) -> p n k", k=TAPS),
                                            AX.X, ALU.add).then_inc(reduced, 1)

                dve.sem_inc(reduced, 1)
                dve.wait_ge(h_t_cleared, 1)
                with dve.Fori(0, CHUNKS) as c:
                    for j in range(CHUNK):
                        if j in (0, HALVES[1][0]):
                            dve.wait_ge(table_written[0 if j == 0 else 1], (c + 1) * 32)
                        sample_h(c, j)
                        if j:
                            offsets(c, j - 1)
                    offsets(c, CHUNK - 1)
                    dve.wait_ge(reduced, (c + 1) * CHUNK + 1)
                    steps = [0]

                    def link_in_chunk(ins):
                        steps[0] += 1
                        ins.then_inc(chain, 1)
                        dve.wait_ge(chain, c * PLAN_STEPS_2 + steps[0])

                    sample_plan(dve, link_in_chunk, gate_ready, om_ready, CHUNK, TAPS, om[:, :, :],
                                c * CHUNK, ds(c * CHUNK * TAPS, CHUNK * TAPS), weights2, index2, c + 1)
                    assert steps[0] == PLAN_STEPS_2, steps
                nth = CHUNKS * CHUNK
                dve.wait_ge(convolved, nth + 1)
                nc.vector.tensor_tensor(
                    prod.rearrange("p (k n) -> p k n", k=TAPS),
                    off_bank(CHUNK).rearrange("p (k n) -> p k n", k=TAPS),
                    inside_sb[:, nth, :].unsqueeze(2).to_broadcast([P, TAPS, N_OFF]), ALU.mult)\
                    .then_inc(masked, 1)
                dve.wait_ge(masked, nth + 1 + 2)
                nc.vector.tensor_reduce(om[:, 0, :], prod.rearrange("p (k n) -> p n k", k=TAPS),
                                        AX.X, ALU.add).then_inc(reduced, 1)
                dve.wait_ge(reduced, nth + 2)
                more = [CHUNKS * PLAN_STEPS_2]

                def link_last(ins):
                    more[0] += 1
                    ins.then_inc(chain, 1)
                    dve.wait_ge(chain, more[0])

                sample_plan(dve, link_last, gate_ready, om_ready, 1, TAPS, om[:, 0:1, :], nth,
                            slice(nth * TAPS, (nth + 1) * TAPS), weights2, index2, CHUNKS + 1)

        with ExitStack() as phase:
            def sem(name):
                return phase.enter_context(nc.semaphore(name))

            x_loaded = [sem("residual_loaded_a"), sem("residual_loaded_b")]
            stored = [sem("stored_a"), sem("stored_b")]
            rows_copied = sem("rows_copied3")
            gathered = [sem(f"gathered3_{g}") for g in range(GROUPS)]
            scaled = sem("scaled")
            summed = sem("summed3")
            sampled = sem("sampled3")
            transposed = sem("transposed")
            hi_ready = sem("hi_ready")
            lo_ready = sem("lo_ready")
            multiplied = sem("multiplied")
            acc_copied = sem("acc_copied")
            biased = sem("biased")
            activated = sem("activated")
            turned = sem("turned")
            finished = sem("finished")
            block = phase.enter_context(nc.Block())

            @block.sync
            def _(sp):
                def load(c, half):
                    j, n = HALVES[half]
                    for image, px, o, count in pieces(c * CHUNK_PX + j * P, n * P):
                        sp.dma_start(stage[:, :, j * P + o:j * P + o + count],
                                     x[image].rearrange("(k p) n -> p k n", p=P)[:, :, px:px + count])\
                            .then_inc(x_loaded[half], 16)

                for half in range(2):
                    load(0, half)
                for c in range(CHUNKS):
                    for half, (j, n) in enumerate(HALVES):
                        sp.wait_ge(finished, c * CHUNK + j + n)
                        for image, px, o, count in pieces(c * CHUNK_PX + j * P, n * P):
                            sp.dma_start(out[image].rearrange("(k p) n -> p k n", p=P)[:, :, px:px + count],
                                         stage[:, :, j * P + o:j * P + o + count])\
                                .then_inc(stored[half], 16)
                        sp.wait_ge(stored[half], (c + 1) * 32)
                        if c + 1 < CHUNKS:
                            load(c + 1, half)

            @block.gpsimd
            def _(pool):
                with pool.Fori(0, TILES) as t:
                    for g in range(GROUPS):
                        pool.wait_ge(sampled, t * GROUPS + g + 1)
                        nc.gpsimd.tensor_copy(row_cur[:, g * GROUP:(g + 1) * GROUP],
                                              index2[:, ds((t + 1) * TAPS + g * GROUP, GROUP)])\
                            .then_inc(rows_copied, 1)
                        pool.wait_ge(rows_copied, t * GROUPS + g + 1)
                        pool.sem_inc(gather_cleared, 1)
                        for k in range(g * GROUP, (g + 1) * GROUP):
                            nc.gpsimd.indirect_dma_start(
                                gather2[:, k, :, :].rearrange("p q c -> p (q c)"), None, table2,
                                bass.IndirectOffsetOnAxis(ap=row_cur[:, k:k + 1], axis=0))\
                                .then_inc(gathered[g], 16)

            def following(t, g):
                return (t, g + 1) if g + 1 < GROUPS else (t + 1, 0)

            def weight(t, k, q):
                return weights2[:, q, ds((t + 1) * TAPS + k, 1)]

            @block.scalar
            def _(act):
                def scale(t, g):
                    act.wait_ge(gathered[g], (t + 1) * 16 * GROUP)
                    act.wait_ge(transposed, t * GROUPS + g + 1)
                    for k in range(GROUP):
                        ins = nc.scalar.activation(val[:, g, k, :], gather2[:, g * GROUP + k, 0, :],
                                                   ACT.Copy, scale=weight(t, g * GROUP + k, 0))
                    ins.then_inc(scaled, 1)

                def upper(t, g):
                    act.wait_ge(transposed, t * GROUPS + g + 1 + GROUPS)
                    act.wait_ge(multiplied, t * GROUPS + g + 1)
                    nc.scalar.activation(val_hi[:, g, :], group_t(g), ACT.Copy).then_inc(hi_ready, 1)

                def copy_acc(t):
                    act.wait_ge(multiplied, (t + 2) * GROUPS)
                    act.wait_ge(biased, t + 1)
                    nc.scalar.activation(acc_sb, psum_acc[:, :], ACT.Copy).then_inc(acc_copied, 1)

                def tile(t, first=False, last=False):
                    for g in range(GROUPS):
                        if not (last and g == GROUPS - 1):
                            scale(*following(t, g))
                        upper(t, g)
                        if g == 0 and not first:
                            copy_acc(t - 1)

                scale(0, 0)
                tile(0, first=True)
                with act.Fori(1, TILES - 1) as t:
                    tile(t)
                tile(TILES - 1, last=True)
                copy_acc(TILES - 1)

            @block.vector
            def _(dve):
                def sample(t, g):
                    dve.wait_ge(scaled, t * GROUPS + g + 1)
                    for q in range(1, 4):
                        for k in range(GROUP):
                            ins = nc.vector.scalar_tensor_tensor(
                                out=val[:, g, k, :], in0=gather2[:, g * GROUP + k, q, :],
                                scalar=weight(t, g * GROUP + k, q), in1=val[:, g, k, :],
                                op0=ALU.mult, op1=ALU.add)
                        if q < 3:
                            ins.then_inc(summed, 1)
                            dve.wait_ge(summed, (t * GROUPS + g) * 2 + q)
                        else:
                            ins.then_inc(sampled, 1)

                def lower(t, g):
                    dve.wait_ge(hi_ready, t * GROUPS + g + 1)
                    dve.wait_ge(multiplied, t * GROUPS + g + 1)
                    nc.vector.tensor_tensor(val_lo[:, g, :], group_t(g), val_hi[:, g, :].bitcast(f32),
                                            ALU.subtract).then_inc(lo_ready, 1)

                def bias_and_relu(t):
                    dve.wait_ge(acc_copied, t + 1)
                    dve.wait_ge(activated, t + 1)
                    nc.vector.tensor_tensor(z_sb, acc_sb, bias2[:, :], ALU.add).then_inc(biased, 1)
                    dve.wait_ge(biased, t + 1 + 1)
                    dve.wait_ge(turned, t + 1)
                    nc.vector.scalar_tensor_tensor(out=z_act, in0=z_sb, scalar=SLOPE, in1=z_sb,
                                                   op0=ALU.mult, op1=ALU.max).then_inc(activated, 1)

                def residual(t, j, half, c):
                    dve.wait_ge(x_loaded[half], (c + 1) * 32)
                    dve.wait_ge(turned, t + 1 + 1)
                    here = stage[:, :, ds(j * P, P)]
                    nc.vector.tensor_tensor(here, psum_out[:, :].rearrange("p (k n) -> p k n", k=KT1),
                                            here, ALU.add).then_inc(finished, 1)

                def tile(t, j_before, first=False, last=False, half=0, c=0):
                    for g in range(GROUPS):
                        if not (last and g == GROUPS - 1):
                            sample(*following(t, g))
                        lower(t, g)
                        if g == 0 and not first:
                            bias_and_relu(t - 1)
                        if g == 1 and not first:
                            residual(t - 1, j_before, half, c)

                dve.sem_inc(sampled, GROUPS)
                dve.sem_inc(lo_ready, GROUPS)
                dve.sem_inc(biased, 1)
                dve.sem_inc(activated, 1)
                sample(0, 0)
                tile(0, 0, first=True)
                def finish_chunk(c, tiles):
                    for half, (j0, n) in enumerate(HALVES):
                        n = min(n, tiles - j0)
                        with dve.Fori(j0, j0 + n) as j:
                            tile(c * CHUNK + j + 1, j, half=half, c=c)

                with dve.Fori(0, CHUNKS - 1) as c:
                    finish_chunk(c, CHUNK)
                finish_chunk(CHUNKS - 1, CHUNK - 2)
                tile(TILES - 1, CHUNK - 2, last=True, half=1, c=CHUNKS - 1)
                bias_and_relu(TILES - 1)
                residual(TILES - 1, CHUNK - 1, 1, CHUNKS - 1)

            @block.tensor
            def _(pe):
                def transpose(t, g):
                    pe.wait_ge(sampled, t * GROUPS + g + 1 + GROUPS)
                    pe.wait_ge(lo_ready, t * GROUPS + g + 1)
                    for k in range(GROUP):
                        for kt in range(KT2):
                            n = (k * KT2 + kt) * P
                            last = nc.tensor.transpose(group_t(g)[:, n:n + P],
                                                       val[:, g, k, kt * P:(kt + 1) * P], ident[:, :])
                    last.then_inc(transposed, 1)

                def multiply(t, g):
                    pe.wait_ge(lo_ready, t * GROUPS + g + 1 + GROUPS)
                    for s in range(GROUP * KT2):
                        slab = g * GROUP * KT2 + s
                        for a, b in ((val_hi, w2_hi), (val_hi, w2_lo), (val_lo, w2_hi)):
                            last = nc.tensor.matmul(
                                psum_acc[:, :], a[:, g, s * P:(s + 1) * P], b[:, slab, :],
                                start=(slab == 0 and b is w2_hi and a is val_hi),
                                stop=(slab == SLABS - 1 and a is val_lo))
                    last.then_inc(multiplied, 1)

                def turn(t):
                    pe.wait_ge(activated, t + 1 + 1)
                    for k in range(KT1):
                        last = nc.tensor.transpose(psum_out[:, k * P:(k + 1) * P],
                                                   z_act[:, k * P:(k + 1) * P], ident[:, :])
                    last.then_inc(turned, 1)

                def tile(t, first=False, last=False):
                    for g in range(GROUPS):
                        if not (last and g == GROUPS - 1):
                            transpose(*following(t, g))
                        if g == 0 and not first:
                            pe.wait_ge(acc_copied, t)
                        if g == 1 and not first:
                            turn(t - 1)
                        multiply(t, g)

                pe.sem_inc(transposed, GROUPS)
                pe.sem_inc(multiplied, GROUPS)
                pe.sem_inc(turned, 1)
                transpose(0, 0)
                tile(0, first=True)
                with pe.Fori(1, TILES - 1) as t:
                    tile(t)
                tile(TILES - 1, last=True)
                turn(TILES - 1)


PLAN_STEPS_1 = 12
PLAN_STEPS_2 = 13


def kernel(**inputs):
    import concourse.bacc as bacc
    from concourse.bass_utils import run_bass_kernel_spmd as run

    a = {k.removeprefix("L0_conv_"): np.asarray(v) for k, v in inputs.items()}
    where, inside, shift = pixel_constants()
    arrays = {
        "x": a["x"].reshape(N_IMAGES, C_OUT, IMAGE),
        "w1": np.concatenate([a["w1"][:, :, 0, 0], a["w_off1"][:, :, 0, 0]]).T,
        "norm1": np.stack([a[n] for n in ("g1", "v1", "m1", "bb1", "b1")]),
        "w_off2": a["w_off2"].transpose(2, 3, 1, 0).reshape(TAPS, C_MID, 3 * TAPS),
        "w2": a["w2"].transpose(2, 3, 1, 0).reshape(TAPS * C_MID, C_OUT),
        "norm2": np.stack([a[n] for n in ("g2", "v2", "m2", "bb2", "b2")]),
        "b_off1": a["b_off1"].reshape(1, 3),
        "b_off2": a["b_off2"].reshape(1, 3 * TAPS),
        "where": where,
        "inside": inside,
        "shift": shift,
        "identity": np.eye(P, dtype=np.float32),
    }
    arrays = {k: np.ascontiguousarray(v) for k, v in arrays.items()}
    nc = bacc.Bacc("TRN2", target_bir_lowering=False, num_devices=1)
    args = [nc.dram_tensor(k, v.shape, mybir.dt.from_np(v.dtype), kind="ExternalInput").ap()
            for k, v in arrays.items()]
    out = nc.dram_tensor("out", (N_IMAGES, C_OUT, IMAGE), mybir.dt.float32, kind="ExternalOutput").ap()
    deformable_kernel(nc, *args, out)
    r = run(nc, [arrays], core_ids=[0])
    return r.results[0]["out"].reshape(N_IMAGES, C_OUT, HEIGHT, WIDTH)
```

```python
from contextlib import ExitStack

import numpy as np

import concourse.bass as bass
from concourse import mybir

N_IMAGES, C_OUT, HEIGHT, WIDTH = 8, 512, 52, 52
C_MID = C_OUT // 2
IMAGE = HEIGHT * WIDTH
P = 128
PIXELS = N_IMAGES * IMAGE
TILES = PIXELS // P
CHUNK = 13
CHUNKS = TILES // CHUNK
CHUNK_PX = CHUNK * P
TAPS = 9
GROUP = 3
GROUPS = TAPS // GROUP
TABLE_ROWS = PIXELS + WIDTH
EPS, SLOPE = 1e-5, 0.1
ROUND = 1.5 * 2.0**23
HALVES = ((0, 6), (6, 7))
BLOCKS = ((0, 3), (3, 3), (6, 3), (9, 2), (11, 2))
DX = 32
SLOTS = 7
TAIL = 2 * P


def pixel_constants():
    g = np.arange(PIXELS)
    y, x, first = g % IMAGE // WIDTH, g % WIDTH, g // IMAGE * IMAGE + WIDTH
    where = np.zeros((TILES + 1, P, 3), np.float32)
    where[0, :, 2] = WIDTH
    where[1:] = np.stack([y, x, first], -1).reshape(TILES, P, 3)
    inside = np.zeros((TILES + 1, P, TAPS), np.float32)
    for k in range(TAPS):
        ty, tx = y + k // 3 - 1, x + k % 3 - 1
        inside[1:, :, k] = ((ty >= 0) & (ty < HEIGHT) & (tx >= 0) & (tx < WIDTH)).reshape(TILES, P)
    shift = np.array([[k // 3 - 1 for k in range(TAPS)] + [k % 3 - 1 for k in range(TAPS)]], np.float32)
    return where.transpose(1, 0, 2).copy(), inside.transpose(1, 0, 2).copy(), shift


def pieces(first, count):
    end = (first // IMAGE + 1) * IMAGE
    cut = end - first if first < end < first + count else count // 2
    return [((first + o) // IMAGE, (first + o) % IMAGE, o, n) for o, n in ((0, cut), (cut, count - cut))]


def deformable_kernel(nc, x, w1, norm1, w_off2, w2, norm2, b_off1, b_off2, where, inside, shift,
                      identity, out):
    f32, f32r = mybir.dt.float32, mybir.dt.float32r
    u32, u16 = mybir.dt.uint32, mybir.dt.uint16
    ALU, ACT, AX = mybir.AluOpType, mybir.ActivationFunctionType, mybir.AxisListType
    ds = bass.ds

    table1 = nc.dram_tensor("table1", [TABLE_ROWS, 2 * C_MID], f32, kind="Internal").ap()
    table2 = nc.dram_tensor("table2", [TABLE_ROWS, 2 * C_MID], f32, kind="Internal").ap()
    KT1 = C_OUT // P
    KT2 = C_MID // P
    N1 = C_MID + 3
    N_OFF = 3 * TAPS
    SLABS = TAPS * KT2
    NORMS = 5

    with ExitStack() as ctx:
        def sb(name, shape, dt=f32):
            return ctx.enter_context(nc.sbuf_tensor(name, shape, dt))

        def ps(name, cols):
            return ctx.enter_context(nc.psum_tensor(name, [P, cols], f32))

        def sem(name):
            return ctx.enter_context(nc.semaphore(name))

        w2_hi = sb("w2_hi", [P, SLABS, C_OUT], f32r)
        w2_lo = sb("w2_lo", [P, SLABS, C_OUT], f32r)
        val_hi = sb("val_hi", [P, GROUPS, GROUP * C_MID], f32r)
        val_lo = sb("val_lo", [P, GROUPS, GROUP * C_MID], f32r)
        weights2 = sb("weights2", [P, 4, (TILES + 1) * TAPS])
        index2 = sb("index2", [P, (TILES + 1) * TAPS], u16)
        bias2 = sb("bias2", [P, C_OUT])
        ident = sb("ident", [P, P])
        boff1 = sb("boff1", [P, 3])
        boff2 = sb("boff2", [P, N_OFF])
        shifts = sb("shifts", [P, 2 * TAPS])
        row_cur = sb("row_cur", [P, 16], u32)

        area_a = sb("area_a", [P, KT1 * CHUNK_PX + KT1 * N1])
        x_sb = area_a[:, 0:KT1 * CHUNK_PX].rearrange("p (k n) -> p k n", k=KT1)
        w1_sb = area_a[:, KT1 * CHUNK_PX:].rearrange("p (k n) -> p k n", k=KT1)
        HT = TAIL + CHUNK_PX + 64
        h_stage = area_a[:, 0:CHUNK * C_MID].rearrange("p (t c) -> p t c", t=CHUNK)
        h_t = area_a[:, CHUNK * C_MID:CHUNK * C_MID + KT2 * HT].rearrange("p (k n) -> p k n", k=KT2)
        stage = x_sb
        area_b = sb("area_b", [P, SLOTS * 4 * C_MID + (TILES + 1) * TAPS + 9 * P])
        HALF_SLABS = SLABS // 2
        w2_raw = area_b[:, 0:HALF_SLABS * C_OUT].rearrange("p (s n) -> p s n", s=HALF_SLABS)
        at = HALF_SLABS * C_OUT
        norm1_sb = area_b[:, at:at + NORMS * C_MID].rearrange("p (v n) -> p v n", v=NORMS)
        at += NORMS * C_MID
        norm2_sb = area_b[:, at:at + NORMS * C_OUT].rearrange("p (v n) -> p v n", v=NORMS)
        gather1 = area_b[:, 0:SLOTS * 4 * C_MID].rearrange("p (s q c) -> p s q c", s=SLOTS, q=4)
        at = SLOTS * 4 * C_MID
        inside_sb = area_b[:, at:at + (TILES + 1) * TAPS].rearrange("p (t k) -> p t k", k=TAPS)
        at += (TILES + 1) * TAPS
        q_sb = area_b[0:3 * DX, at:at + 9 * P].rearrange("p (y n) -> p y n", y=3)
        gather2 = area_b[:, 0:TAPS * 4 * C_MID].rearrange("p (s q c) -> p s q c", s=TAPS, q=4)
        y_stage = weights2[:, :, :].rearrange("p q n -> p (q n)")[:, 0:CHUNK * N1]\
            .rearrange("p (t c) -> p t c", t=CHUNK)
        C_SIZE = 4326
        area_c = sb("area_c", [P, C_SIZE])
        at = 0

        def part(n):
            nonlocal at
            at += n
            assert at <= C_SIZE, at
            return area_c[:, at - n:at]

        woff_sb = part(KT2 * TAPS * DX).rearrange("p (k y n) -> p k y n", k=KT2, y=3)
        weights1 = part(4 * TILES).rearrange("p (q t) -> p q t", q=4)
        index1 = part(TILES)
        bias1 = part(C_MID)
        where_sb = part((TILES + 1) * 3).rearrange("p (t v) -> p t v", v=3)
        om = part(CHUNK * N_OFF).rearrange("p (t n) -> p t n", t=CHUNK)
        spot = part(CHUNK * 2 * TAPS)
        corner = part(CHUNK * 2 * TAPS)
        near = part(CHUNK * 2 * TAPS)
        far = part(CHUNK * 2 * TAPS)
        gate = part(CHUNK * TAPS)
        prod = part(3 * TAPS * N_OFF)
        at = 0
        val = part(TAPS * C_MID).rearrange("p (g k c) -> p g k c", g=GROUPS, k=GROUP)
        acc_sb = part(C_OUT)
        z_sb = part(C_OUT)
        z_act = part(C_OUT)

        psum_t = ps("psum_t", 8 * 512)
        psum_acc = psum_t[:, 6 * 512:7 * 512]
        psum_out = psum_t[:, 7 * 512:]

        gather_cleared = sem("gather_cleared")

        def group_t(g):
            return psum_t[:, 1024 * g:1024 * g + GROUP * C_MID]

        def sample_plan(dve, link, gate_ready, om_ready, tiles, k, raw, slot, base, wts, rows,
                        gate_count):
            n = tiles * 2 * k
            o = om[:, 0:tiles, 0:3 * k]

            def two(t):
                return t[:, 0:n].rearrange("p (t v) -> p t v", t=tiles)

            def axis(t, a):
                return two(t)[:, :, a * k:(a + 1) * k]

            b_off = (boff1 if k == 1 else boff2)[:, 0:3 * k]
            yx = where_sb[:, ds(slot, tiles), 0:2]
            first = where_sb[:, ds(slot, tiles), 2:3]
            m = gate[:, 0:tiles * k].rearrange("p (t k) -> p t k", k=k)
            nc.vector.tensor_tensor(o, raw, b_off.unsqueeze(1).to_broadcast([P, tiles, 3 * k]), ALU.add)\
                .then_inc(om_ready, 1)
            dve.wait_ge(om_ready, gate_count + 1)
            if k == 1:
                link(nc.vector.tensor_tensor(two(spot), o[:, :, 0:2], yx, ALU.add))
            else:
                for a in range(2):
                    last = nc.vector.tensor_tensor(
                        axis(spot, a), yx[:, :, a:a + 1].to_broadcast([P, tiles, k]),
                        shifts[:, a * k:(a + 1) * k].unsqueeze(1).to_broadcast([P, tiles, k]), ALU.add)
                link(last)
                link(nc.vector.tensor_tensor(two(spot), o[:, :, 0:2 * k], two(spot), ALU.add))
            link(nc.vector.tensor_scalar(two(corner), two(spot), 0.0, float(HEIGHT - 1), ALU.max, ALU.min))
            link(nc.vector.tensor_scalar(two(corner), two(corner), -0.5, ROUND, ALU.add, ALU.add))
            link(nc.vector.tensor_scalar(two(corner), two(corner), ROUND, None, ALU.subtract))
            link(nc.vector.tensor_tensor(two(spot), two(spot), two(corner), ALU.subtract))
            link(nc.vector.tensor_scalar(two(near), two(spot), -1.0, 1.0, ALU.mult, ALU.add))
            link(nc.vector.scalar_tensor_tensor(out=two(near), in0=two(spot), scalar=1.0, in1=two(near),
                                                op0=ALU.add, op1=ALU.min))
            link(nc.vector.tensor_scalar(two(far), two(spot), -1.0, 2.0, ALU.mult, ALU.add))
            link(nc.vector.scalar_tensor_tensor(out=two(far), in0=two(far), scalar=0.0, in1=two(spot),
                                                op0=ALU.max, op1=ALU.min))
            dve.wait_ge(gate_ready, gate_count)
            for t in (near, far):
                last = nc.vector.scalar_tensor_tensor(out=axis(t, 0), in0=axis(t, 0), scalar=0.0, in1=m,
                                                      op0=ALU.max, op1=ALU.mult)
            link(last)
            for q, (ty, tx) in enumerate(((near, near), (far, near), (near, far), (far, far))):
                nc.vector.scalar_tensor_tensor(
                    out=wts[:, q, base].rearrange("p (t k) -> p t k", k=k), in0=axis(tx, 1), scalar=0.0,
                    in1=axis(ty, 0), op0=ALU.max, op1=ALU.mult)
            link(nc.vector.scalar_tensor_tensor(out=axis(spot, 0), in0=axis(corner, 0), scalar=float(WIDTH),
                                                in1=axis(corner, 1), op0=ALU.mult, op1=ALU.add))
            link(nc.vector.tensor_tensor(rows[:, base].rearrange("p (t k) -> p t k", k=k), axis(spot, 0),
                                         first.to_broadcast([P, tiles, k]), ALU.add))

        def linker(dve, done):
            count = [0]

            def link(ins):
                count[0] += 1
                ins.then_inc(done, 1)
                dve.wait_ge(done, count[0])
            return link, count

        def table_writes(eng, table, source, c, half, written):
            j, n = HALVES[half]
            for row, col in ((WIDTH, 0), (0, C_MID)):
                dst = table[ds(c * CHUNK_PX + row + j * P, n * P), col:col + C_MID]
                eng.dma_start(dst.rearrange("(t p) c -> p t c", p=P), source[:, j:j + n, 0:C_MID])\
                    .then_inc(written, 16)

        with ExitStack() as phase:
            def sem(name):
                return phase.enter_context(nc.semaphore(name))

            const_loaded = sem("const_loaded")
            x_loaded = [sem("x_loaded_a"), sem("x_loaded_b")]
            raw_loaded = [sem("raw_loaded_a"), sem("raw_loaded_b")]
            x_used = sem("x_used")
            y_copied = sem("y_copied")
            table_written = [sem("table_written_a"), sem("table_written_b")]
            root_ready = sem("root_ready")
            var_ready = sem("var_ready")
            edge_cleared = sem("edge_cleared")
            edge_written = sem("edge_written")
            w1_scaled = sem("w1_scaled")
            w2_split = sem("w2_split")
            om_ready = sem("om_ready")
            gate_ready = sem("gate_ready")
            chain = sem("chain")
            setup = sem("setup")
            block = phase.enter_context(nc.Block())
            CONSTS = 10

            def y_bank(j):
                b = j % 7
                return psum_acc[:, 0:N1] if b == 6 else psum_t[:, 512 * b:512 * b + N1]

            @block.sync
            def _(sp):
                sp.dma_start(w1_sb, w1.rearrange("(k p) n -> p k n", p=P)).then_inc(const_loaded, 16)
                sp.dma_start(norm1_sb, norm1.unsqueeze(0).to_broadcast([P, NORMS, C_MID]))\
                    .then_inc(const_loaded, 16)
                for c in range(CHUNKS):
                    for half, (j, n) in enumerate(HALVES):
                        if c:
                            sp.wait_ge(x_used, CHUNK * (c - 1) + j + n)
                        for image, px, o, count in pieces(c * CHUNK_PX + j * P, n * P):
                            sp.dma_start(x_sb[:, :, j * P + o:j * P + o + count],
                                         x[image].rearrange("(k p) n -> p k n", p=P)[:, :, px:px + count])\
                                .then_inc(x_loaded[half], 16)
                    if c == 0:
                        for dst, src in (
                            (norm2_sb, norm2.unsqueeze(0).to_broadcast([P, NORMS, C_OUT])),
                            (boff1[:, :], b_off1.to_broadcast([P, 3])),
                            (boff2[:, :], b_off2.to_broadcast([P, N_OFF])),
                            (shifts[:, :], shift.to_broadcast([P, 2 * TAPS])),
                            (ident[:, :], identity),
                            (where_sb, where),
                        ):
                            sp.dma_start(dst, src).then_inc(const_loaded, 16)
                        for k in range(KT2):
                            sp.dma_start(woff_sb[:, k, :, :],
                                         w_off2[:, k * P:(k + 1) * P, :].rearrange("y p n -> p y n"))\
                                .then_inc(const_loaded, 16)

            @block.gpsimd
            def _(pool):
                nc.gpsimd.memset(prod[:, 0:C_MID], 0.0).then_inc(edge_cleared, 1)
                pool.wait_ge(edge_cleared, 1)
                for table in (table1, table2):
                    for row, col in ((0, 0), (PIXELS, C_MID)):
                        pool.dma_start(table[row:row + WIDTH, col:col + C_MID], prod[0:WIDTH, 0:C_MID])\
                            .then_inc(edge_written, 16)
                for part_no in range(2):
                    if part_no:
                        pool.wait_ge(w2_split, HALF_SLABS)
                    pool.dma_start(w2_raw, w2[part_no * HALF_SLABS * P:(part_no + 1) * HALF_SLABS * P, :]
                                   .rearrange("(s p) n -> p s n", p=P)).then_inc(raw_loaded[part_no], 16)
                pool.wait_ge(edge_written, 64)

            @block.tensor
            def _(pe):
                pe.wait_ge(w1_scaled, 1)
                with pe.Fori(0, CHUNKS) as c:
                    for half, (j0, n) in enumerate(HALVES):
                        pe.wait_ge(x_loaded[half], (c + 1) * 32)
                        for j in range(j0, j0 + n):
                            pe.wait_ge(y_copied, c * CHUNK + j + 1)
                            for k in range(KT1):
                                last = nc.tensor.matmul(y_bank(j),
                                                        x_sb[:, k, j * P:(j + 1) * P], w1_sb[:, k, :],
                                                        start=(k == 0), stop=(k == KT1 - 1))
                            last.then_inc(x_used, 1)

            @block.scalar
            def _(act):
                for layer, norm in ((0, norm1_sb), (1, norm2_sb)):
                    act.wait_ge(var_ready, layer + 1)
                    nc.scalar.activation(norm[:, 1, :], norm[:, 1, :], ACT.Sqrt).then_inc(root_ready, 1)
                act.sem_inc(y_copied, 6)
                for half in range(2):
                    act.sem_inc(table_written[half], 32)
                with act.Fori(0, CHUNKS) as c:
                    for half, (j0, n) in enumerate(HALVES):
                        act.wait_ge(table_written[half], (c + 1) * 32)
                        act.wait_ge(om_ready, c + 1)
                        for j in range(j0, j0 + n):
                            act.wait_ge(x_used, c * CHUNK + j + 1)
                            nc.scalar.activation(y_stage[:, j, :], y_bank(j), ACT.Copy).then_inc(y_copied, 1)
                        act.wait_ge(y_copied, c * CHUNK + 6 + j0 + n)
                        table_writes(act, table1, y_stage, c, half, table_written[half])
                    act.wait_ge(om_ready, c + 2)
                    nc.scalar.activation(gate[:, 0:CHUNK].unsqueeze(2), om[:, :, 2:3], ACT.Sigmoid)\
                        .then_inc(gate_ready, 1)
                for half in range(2):
                    act.wait_ge(table_written[half], (CHUNKS + 1) * 32)

            @block.vector
            def _(dve):
                link, count = linker(dve, setup)

                def fold(norm, bias):
                    link(nc.vector.reciprocal(norm[:, 1, :], norm[:, 1, :]))
                    link(nc.vector.tensor_tensor(norm[:, 0, :], norm[:, 0, :], norm[:, 1, :], ALU.mult))
                    link(nc.vector.tensor_tensor(bias, norm[:, 4, :], norm[:, 2, :], ALU.subtract))
                    link(nc.vector.tensor_tensor(bias, bias, norm[:, 0, :], ALU.mult))
                    link(nc.vector.tensor_tensor(bias, bias, norm[:, 3, :], ALU.add))

                dve.sem_inc(om_ready, 1)
                dve.wait_ge(const_loaded, 16 * CONSTS)
                for norm in (norm1_sb, norm2_sb):
                    nc.vector.tensor_scalar(norm[:, 1, :], norm[:, 1, :], EPS, None, ALU.add)\
                        .then_inc(var_ready, 1)
                dve.wait_ge(root_ready, 1)
                fold(norm1_sb, bias1)
                for k in range(KT1):
                    last = nc.vector.tensor_tensor(w1_sb[:, k, 0:C_MID], w1_sb[:, k, 0:C_MID],
                                                   norm1_sb[:, 0, :], ALU.mult)
                last.then_inc(w1_scaled, 1)
                dve.wait_ge(root_ready, 2)
                fold(norm2_sb, bias2[:, :])

                def split(part_no):
                    dve.wait_ge(raw_loaded[part_no], 16)
                    for s in range(HALF_SLABS):
                        hi = w2_hi[:, part_no * HALF_SLABS + s, :]
                        lo = w2_lo[:, part_no * HALF_SLABS + s, :]
                        link(nc.vector.tensor_tensor(w2_raw[:, s, :], w2_raw[:, s, :], norm2_sb[:, 0, :],
                                                     ALU.mult))
                        link(nc.vector.tensor_copy(hi, w2_raw[:, s, :]))
                        nc.vector.tensor_tensor(lo, w2_raw[:, s, :], hi.bitcast(f32), ALU.subtract)\
                            .then_inc(w2_split, 1)

                def plan_chunk(c):
                    dve.wait_ge(y_copied, (c + 1) * CHUNK + 6)
                    steps = [0]

                    def link_in_chunk(ins):
                        steps[0] += 1
                        ins.then_inc(chain, 1)
                        dve.wait_ge(chain, c * PLAN_STEPS_1 + steps[0])

                    sample_plan(dve, link_in_chunk, gate_ready, om_ready, CHUNK, 1,
                                y_stage[:, :, C_MID:], c * CHUNK + 1, ds(c * CHUNK, CHUNK), weights1,
                                index1, c + 1)
                    assert steps[0] == PLAN_STEPS_1, steps

                split(0)
                plan_chunk(0)
                split(1)
                with dve.Fori(1, CHUNKS) as c:
                    plan_chunk(c)

        with ExitStack() as phase:
            def sem(name):
                return phase.enter_context(nc.semaphore(name))

            inside_loaded = sem("inside_loaded")
            h_t_cleared = sem("h_t_cleared")
            rows_copied = sem("rows_copied")
            gathered = [sem(f"gathered1_{s}") for s in range(SLOTS)]
            sampled = sem("sampled")
            summed = sem("summed")
            h_ready = sem("h_ready")
            h_transposed = sem("h_transposed")
            h_t_ready = sem("h_t_ready")
            tail_kept = sem("tail_kept")
            convolved = sem("convolved")
            conv_copied = sem("conv_copied")
            conv_turned = sem("conv_turned")
            masked = sem("masked")
            reduced = sem("reduced")
            table_written = [sem("table2_written_a"), sem("table2_written_b")]
            om_ready = sem("om2_ready")
            gate_ready = sem("gate2_ready")
            chain = sem("chain2")
            block = phase.enter_context(nc.Block())
            LAST_BLOCK = len(BLOCKS) - 1
            FINAL = (0, 1)

            def t_bank(j):
                b = 512 * (j % 3 if j < CHUNK - 2 else j - (CHUNK - 2))
                return psum_t[:, b:b + C_MID]

            def conv_bank(u, n):
                b = 512 * (3 + u % 2)
                return psum_t[0:3 * DX, b:b + n * P + 2]

            def off_bank(i):
                return off_banks[:, i, :]

            off_banks = psum_t[:, 512 * 5:].rearrange("p (t n) -> p t n", t=3)

            @block.sync
            def _(sp):
                sp.dma_start(inside_sb, inside).then_inc(inside_loaded, 16)
                sp.wait_ge(inside_loaded, 16)

            @block.gpsimd
            def _(pool):
                with pool.Fori(0, CHUNKS) as c:
                    for half, (j0, n) in enumerate(HALVES):
                        pool.wait_ge(sampled, c * CHUNK + j0 + n)
                        nc.gpsimd.tensor_copy(row_cur[:, j0:j0 + n], index1[:, ds(c * CHUNK + j0, n)])\
                            .then_inc(rows_copied, 1)
                        pool.wait_ge(rows_copied, 2 * c + half + 1)
                        for j in range(j0, j0 + n):
                            back = SLOTS if j >= SLOTS else CHUNK if j + SLOTS >= CHUNK else CHUNK - SLOTS
                            pool.wait_ge(sampled, c * CHUNK + j + 1 - back + CHUNK)
                            pool.sem_inc(gather_cleared, 1)
                            nc.gpsimd.indirect_dma_start(
                                gather1[:, j % SLOTS, :, :].rearrange("p q c -> p (q c)"), None,
                                table1, bass.IndirectOffsetOnAxis(ap=row_cur[:, j:j + 1], axis=0))\
                                .then_inc(gathered[j % SLOTS], 16)

            @block.tensor
            def _(pe):
                def transpose_h(c, b):
                    j0, n = BLOCKS[b]
                    for j in range(j0, j0 + n):
                        pe.wait_ge(h_ready, c * CHUNK + j + 1)
                        pe.wait_ge(h_t_ready, c * CHUNK + j + 1)
                        for kt in range(KT2):
                            last = nc.tensor.transpose(t_bank(j)[:, kt * P:(kt + 1) * P],
                                                       h_stage[:, j, kt * P:(kt + 1) * P], ident[:, :])
                        last.then_inc(h_transposed, 1)

                def convolve(c, b, block):
                    j0, n = block
                    for y in range(3):
                        u = 3 * b + y
                        pe.wait_ge(conv_copied, c * 3 * len(BLOCKS) + u + (1 if u else 2))
                        at = TAIL + (j0 - 1) * P - 1 + (y - 1) * WIDTH
                        for kt in range(KT2):
                            last = nc.tensor.matmul(conv_bank(u, n), woff_sb[:, kt, y, :],
                                                    h_t[:, kt, at:at + n * P + 2],
                                                    start=(kt == 0), stop=(kt == KT2 - 1))
                        last.then_inc(convolved, 1)

                def turn_conv(c, b, block):
                    j0, n = block
                    pe.wait_ge(conv_copied, (c * len(BLOCKS) + b + 1) * 3 + 2)
                    pe.wait_ge(masked, c * len(BLOCKS) + b + 1)
                    for i in range(n):
                        for y in range(3):
                            last = nc.tensor.transpose(off_bank(i)[:, y * 3 * DX:(y + 1) * 3 * DX],
                                                       q_sb[:, y, i * P:(i + 1) * P],
                                                       ident[0:3 * DX, 0:3 * DX])
                    last.then_inc(conv_turned, 1)

                def chunk(c, first=False):
                    for b, blk in enumerate(BLOCKS):
                        transpose_h(c, b)
                        if b:
                            turn_conv(c, b - 1, BLOCKS[b - 1])
                        elif not first:
                            turn_conv(c - 1, LAST_BLOCK, BLOCKS[LAST_BLOCK])
                        j0, n = blk
                        pe.wait_ge(h_t_ready, c * CHUNK + j0 + n + 2)
                        if b == 0:
                            pe.wait_ge(tail_kept, c + 1)
                        convolve(c, b, blk)

                chunk(0, first=True)
                with pe.Fori(1, CHUNKS) as c:
                    chunk(c)
                turn_conv(CHUNKS - 1, LAST_BLOCK, BLOCKS[LAST_BLOCK])
                pe.wait_ge(tail_kept, CHUNKS + 1)
                convolve(CHUNKS, 0, FINAL)
                turn_conv(CHUNKS, 0, FINAL)

            @block.scalar
            def _(act):
                act.sem_inc(h_t_ready, 2)
                act.sem_inc(conv_copied, 2)
                for half in range(2):
                    act.sem_inc(table_written[half], 32)
                act.wait_ge(h_t_cleared, 1)
                act.sem_inc(tail_kept, 1)

                def copy_h_t(c, b):
                    j0, n = BLOCKS[b]
                    for j in range(j0, j0 + n):
                        act.wait_ge(h_transposed, c * CHUNK + j + 1)
                        nc.scalar.activation(h_t[:, :, TAIL + j * P:TAIL + (j + 1) * P],
                                             t_bank(j).rearrange("p (k n) -> p k n", k=KT2),
                                             ACT.Copy).then_inc(h_t_ready, 1)

                def copy_conv(c, b, block):
                    j0, n = block
                    act.wait_ge(conv_turned, c * len(BLOCKS) + b + 1)
                    for y in range(3):
                        act.wait_ge(convolved, (c * len(BLOCKS) + b) * 3 + y + 1)
                        for dx in range(3):
                            rows = slice(dx * DX, (dx + 1) * DX)
                            last = nc.scalar.activation(q_sb[rows, y, 0:n * P],
                                                        conv_bank(3 * b + y, n)[rows, dx:dx + n * P],
                                                        ACT.Copy)
                        last.then_inc(conv_copied, 1)

                def modulation(count, tiles):
                    act.wait_ge(om_ready, count)
                    nc.scalar.activation(gate[:, 0:tiles * TAPS].rearrange("p (t k) -> p t k", k=TAPS),
                                         om[:, 0:tiles, 2 * TAPS:], ACT.Sigmoid).then_inc(gate_ready, 1)

                def chunk(c, first=False):
                    for b, blk in enumerate(BLOCKS):
                        copy_h_t(c, b)
                        copy_conv(c, b, blk)
                        if b == 0 and not first:
                            modulation(c + 1, CHUNK)
                        for half, (j0, n) in enumerate(HALVES):
                            if blk[0] + blk[1] == j0 + n:
                                act.wait_ge(h_ready, c * CHUNK + j0 + n)
                                table_writes(act, table2, h_stage, c, half, table_written[half])
                    act.wait_ge(h_t_ready, (c + 1) * CHUNK + 2)
                    nc.scalar.activation(h_t[:, :, 0:TAIL], h_t[:, :, CHUNK_PX:CHUNK_PX + TAIL],
                                         ACT.Copy).then_inc(tail_kept, 1)

                chunk(0, first=True)
                with act.Fori(1, CHUNKS) as c:
                    chunk(c)
                modulation(CHUNKS + 1, CHUNK)
                copy_conv(CHUNKS, 0, FINAL)
                act.wait_ge(gate_ready, CHUNKS)
                modulation(CHUNKS + 2, 1)
                for half in range(2):
                    act.wait_ge(table_written[half], (CHUNKS + 1) * 32)

            @block.vector
            def _(dve):
                nc.vector.memset(h_t, 0.0).then_inc(h_t_cleared, 1)
                dve.sem_inc(sampled, CHUNK)
                dve.sem_inc(masked, 1)
                dve.sem_inc(reduced, 1)
                dve.sem_inc(om_ready, 1)
                dve.sem_inc(conv_turned, 1)
                dve.wait_ge(inside_loaded, 16)
                dve.wait_ge(h_t_cleared, 1)

                def sample_h(c, b):
                    j0, n = BLOCKS[b]
                    for half in range(2):
                        if j0 == HALVES[half][0]:
                            dve.wait_ge(table_written[half], (c + 1) * 32)
                    for q in range(4):
                        for j in range(j0, j0 + n):
                            nth = c * CHUNK + j
                            if q == 0:
                                uses = 2 if j + SLOTS < CHUNK or j >= SLOTS else 1
                                dve.wait_ge(gathered[j % SLOTS], (c * uses + (1 if j >= SLOTS else 0) + 1) * 16)
                            v = h_stage[:, j, :]
                            ins = nc.vector.scalar_tensor_tensor(
                                out=v, in0=gather1[:, j % SLOTS, q, :], scalar=weights1[:, q, ds(nth, 1)],
                                in1=bias1 if q == 0 else v, op0=ALU.mult, op1=ALU.add)
                            if q == 3:
                                ins.then_inc(sampled, 1)
                        if q < 3:
                            ins.then_inc(summed, 1)
                            dve.wait_ge(summed, (c * len(BLOCKS) + b) * 3 + q + 1)
                    dve.wait_ge(sampled, c * CHUNK + j0 + n + CHUNK)
                    for j in range(j0, j0 + n):
                        v = h_stage[:, j, :]
                        nc.vector.scalar_tensor_tensor(out=v, in0=v, scalar=SLOPE, in1=v, op0=ALU.mult,
                                                       op1=ALU.max).then_inc(h_ready, 1)

                def offsets(c, b, block):
                    j0, n = block
                    nth = c * len(BLOCKS) + b
                    dve.wait_ge(conv_turned, nth + 2)
                    dve.wait_ge(reduced, nth + 1)
                    nc.vector.tensor_tensor(
                        prod[:, 0:n * TAPS * N_OFF].rearrange("p (t k n) -> p t k n", t=n, k=TAPS),
                        off_banks[:, 0:n, 0:TAPS * DX].rearrange("p t (k n) -> p t k n", k=TAPS)[:, :, :, 0:N_OFF],
                        inside_sb[:, ds(c * CHUNK + j0, n), :].unsqueeze(3).to_broadcast([P, n, TAPS, N_OFF]),
                        ALU.mult).then_inc(masked, 1)
                    dve.wait_ge(masked, nth + 2)
                    nc.vector.tensor_reduce(
                        om[:, j0:j0 + n, :],
                        prod[:, 0:n * TAPS * N_OFF].rearrange("p (t k n) -> p t n k", t=n, k=TAPS),
                        AX.X, ALU.add).then_inc(reduced, 1)

                def plan_chunk(c, tiles, base):
                    dve.wait_ge(reduced, (c * len(BLOCKS) + (len(BLOCKS) if tiles > 1 else 1)) + 1)
                    steps = [0]

                    def link_in_chunk(ins):
                        steps[0] += 1
                        ins.then_inc(chain, 1)
                        dve.wait_ge(chain, c * PLAN_STEPS_2 + steps[0])

                    sample_plan(dve, link_in_chunk, gate_ready, om_ready, tiles, TAPS, om[:, 0:tiles, :],
                                c * CHUNK, base, weights2, index2, c + 1)
                    assert steps[0] == PLAN_STEPS_2, steps

                def chunk(c, first=False):
                    for b, blk in enumerate(BLOCKS):
                        sample_h(c, b)
                        if b:
                            offsets(c, b - 1, BLOCKS[b - 1])
                        elif not first:
                            offsets(c - 1, LAST_BLOCK, BLOCKS[LAST_BLOCK])
                            plan_chunk(c - 1, CHUNK, ds((c - 1) * CHUNK * TAPS, CHUNK * TAPS))

                chunk(0, first=True)
                with dve.Fori(1, CHUNKS) as c:
                    chunk(c)
                offsets(CHUNKS - 1, LAST_BLOCK, BLOCKS[LAST_BLOCK])
                plan_chunk(CHUNKS - 1, CHUNK, ds((CHUNKS - 1) * CHUNK * TAPS, CHUNK * TAPS))
                offsets(CHUNKS, 0, FINAL)
                plan_chunk(CHUNKS, 1, ds(CHUNKS * CHUNK * TAPS, TAPS))

        with ExitStack() as phase:
            def sem(name):
                return phase.enter_context(nc.semaphore(name))

            x_loaded = [sem("residual_loaded_a"), sem("residual_loaded_b")]
            stored = [sem("stored_a"), sem("stored_b")]
            rows_copied = sem("rows_copied3")
            gathered = [sem(f"gathered3_{g}") for g in range(GROUPS)]
            scaled = sem("scaled")
            summed = sem("summed3")
            sampled = sem("sampled3")
            transposed = sem("transposed")
            hi_ready = sem("hi_ready")
            lo_ready = sem("lo_ready")
            multiplied = sem("multiplied")
            acc_copied = sem("acc_copied")
            biased = sem("biased")
            activated = sem("activated")
            turned = sem("turned")
            finished = sem("finished")
            block = phase.enter_context(nc.Block())

            @block.sync
            def _(sp):
                def load(c, half):
                    j, n = HALVES[half]
                    for image, px, o, count in pieces(c * CHUNK_PX + j * P, n * P):
                        sp.dma_start(stage[:, :, j * P + o:j * P + o + count],
                                     x[image].rearrange("(k p) n -> p k n", p=P)[:, :, px:px + count])\
                            .then_inc(x_loaded[half], 16)

                for half in range(2):
                    load(0, half)
                for c in range(CHUNKS):
                    for half, (j, n) in enumerate(HALVES):
                        sp.wait_ge(finished, c * CHUNK + j + n)
                        for image, px, o, count in pieces(c * CHUNK_PX + j * P, n * P):
                            sp.dma_start(out[image].rearrange("(k p) n -> p k n", p=P)[:, :, px:px + count],
                                         stage[:, :, j * P + o:j * P + o + count])\
                                .then_inc(stored[half], 16)
                        sp.wait_ge(stored[half], (c + 1) * 32)
                        if c + 1 < CHUNKS:
                            load(c + 1, half)

            @block.gpsimd
            def _(pool):
                with pool.Fori(0, TILES) as t:
                    for g in range(GROUPS):
                        pool.wait_ge(sampled, t * GROUPS + g + 1)
                        nc.gpsimd.tensor_copy(row_cur[:, g * GROUP:(g + 1) * GROUP],
                                              index2[:, ds((t + 1) * TAPS + g * GROUP, GROUP)])\
                            .then_inc(rows_copied, 1)
                        pool.wait_ge(rows_copied, t * GROUPS + g + 1)
                        pool.sem_inc(gather_cleared, 1)
                        for k in range(g * GROUP, (g + 1) * GROUP):
                            nc.gpsimd.indirect_dma_start(
                                gather2[:, k, :, :].rearrange("p q c -> p (q c)"), None, table2,
                                bass.IndirectOffsetOnAxis(ap=row_cur[:, k:k + 1], axis=0))\
                                .then_inc(gathered[g], 16)

            def following(t, g):
                return (t, g + 1) if g + 1 < GROUPS else (t + 1, 0)

            def weight(t, k, q):
                return weights2[:, q, ds((t + 1) * TAPS + k, 1)]

            @block.scalar
            def _(act):
                def scale(t, g):
                    act.wait_ge(gathered[g], (t + 1) * 16 * GROUP)
                    act.wait_ge(transposed, t * GROUPS + g + 1)
                    for k in range(GROUP):
                        ins = nc.scalar.activation(val[:, g, k, :], gather2[:, g * GROUP + k, 0, :],
                                                   ACT.Copy, scale=weight(t, g * GROUP + k, 0))
                    ins.then_inc(scaled, 1)

                def upper(t, g):
                    act.wait_ge(transposed, t * GROUPS + g + 1 + GROUPS)
                    act.wait_ge(multiplied, t * GROUPS + g + 1)
                    nc.scalar.activation(val_hi[:, g, :], group_t(g), ACT.Copy).then_inc(hi_ready, 1)

                def copy_acc(t):
                    act.wait_ge(multiplied, (t + 2) * GROUPS)
                    act.wait_ge(biased, t + 1)
                    nc.scalar.activation(acc_sb, psum_acc[:, :], ACT.Copy).then_inc(acc_copied, 1)

                def tile(t, first=False, last=False):
                    for g in range(GROUPS):
                        if not (last and g == GROUPS - 1):
                            scale(*following(t, g))
                        upper(t, g)
                        if g == 0 and not first:
                            copy_acc(t - 1)

                scale(0, 0)
                tile(0, first=True)
                with act.Fori(1, TILES - 1) as t:
                    tile(t)
                tile(TILES - 1, last=True)
                copy_acc(TILES - 1)

            @block.vector
            def _(dve):
                def sample(t, g):
                    dve.wait_ge(scaled, t * GROUPS + g + 1)
                    for q in range(1, 4):
                        for k in range(GROUP):
                            ins = nc.vector.scalar_tensor_tensor(
                                out=val[:, g, k, :], in0=gather2[:, g * GROUP + k, q, :],
                                scalar=weight(t, g * GROUP + k, q), in1=val[:, g, k, :],
                                op0=ALU.mult, op1=ALU.add)
                        if q < 3:
                            ins.then_inc(summed, 1)
                            dve.wait_ge(summed, (t * GROUPS + g) * 2 + q)
                        else:
                            ins.then_inc(sampled, 1)

                def lower(t, g):
                    dve.wait_ge(hi_ready, t * GROUPS + g + 1)
                    dve.wait_ge(multiplied, t * GROUPS + g + 1)
                    nc.vector.tensor_tensor(val_lo[:, g, :], group_t(g), val_hi[:, g, :].bitcast(f32),
                                            ALU.subtract).then_inc(lo_ready, 1)

                def bias_and_relu(t):
                    dve.wait_ge(acc_copied, t + 1)
                    dve.wait_ge(activated, t + 1)
                    nc.vector.tensor_tensor(z_sb, acc_sb, bias2[:, :], ALU.add).then_inc(biased, 1)
                    dve.wait_ge(biased, t + 1 + 1)
                    dve.wait_ge(turned, t + 1)
                    nc.vector.scalar_tensor_tensor(out=z_act, in0=z_sb, scalar=SLOPE, in1=z_sb,
                                                   op0=ALU.mult, op1=ALU.max).then_inc(activated, 1)

                def residual(t, j, half, c):
                    dve.wait_ge(x_loaded[half], (c + 1) * 32)
                    dve.wait_ge(turned, t + 1 + 1)
                    here = stage[:, :, ds(j * P, P)]
                    nc.vector.tensor_tensor(here, psum_out[:, :].rearrange("p (k n) -> p k n", k=KT1),
                                            here, ALU.add).then_inc(finished, 1)

                def tile(t, j_before, first=False, last=False, half=0, c=0):
                    for g in range(GROUPS):
                        if not (last and g == GROUPS - 1):
                            sample(*following(t, g))
                        lower(t, g)
                        if g == 0 and not first:
                            bias_and_relu(t - 1)
                        if g == 1 and not first:
                            residual(t - 1, j_before, half, c)

                dve.sem_inc(sampled, GROUPS)
                dve.sem_inc(lo_ready, GROUPS)
                dve.sem_inc(biased, 1)
                dve.sem_inc(activated, 1)
                sample(0, 0)
                tile(0, 0, first=True)
                def finish_chunk(c, tiles):
                    for half, (j0, n) in enumerate(HALVES):
                        n = min(n, tiles - j0)
                        with dve.Fori(j0, j0 + n) as j:
                            tile(c * CHUNK + j + 1, j, half=half, c=c)

                with dve.Fori(0, CHUNKS - 1) as c:
                    finish_chunk(c, CHUNK)
                finish_chunk(CHUNKS - 1, CHUNK - 2)
                tile(TILES - 1, CHUNK - 2, last=True, half=1, c=CHUNKS - 1)
                bias_and_relu(TILES - 1)
                residual(TILES - 1, CHUNK - 1, 1, CHUNKS - 1)

            @block.tensor
            def _(pe):
                def transpose(t, g):
                    pe.wait_ge(sampled, t * GROUPS + g + 1 + GROUPS)
                    pe.wait_ge(lo_ready, t * GROUPS + g + 1)
                    for k in range(GROUP):
                        for kt in range(KT2):
                            n = (k * KT2 + kt) * P
                            last = nc.tensor.transpose(group_t(g)[:, n:n + P],
                                                       val[:, g, k, kt * P:(kt + 1) * P], ident[:, :])
                    last.then_inc(transposed, 1)

                def multiply(t, g):
                    pe.wait_ge(lo_ready, t * GROUPS + g + 1 + GROUPS)
                    for s in range(GROUP * KT2):
                        slab = g * GROUP * KT2 + s
                        for a, b in ((val_hi, w2_hi), (val_hi, w2_lo), (val_lo, w2_hi)):
                            last = nc.tensor.matmul(
                                psum_acc[:, :], a[:, g, s * P:(s + 1) * P], b[:, slab, :],
                                start=(slab == 0 and b is w2_hi and a is val_hi),
                                stop=(slab == SLABS - 1 and a is val_lo))
                    last.then_inc(multiplied, 1)

                def turn(t):
                    pe.wait_ge(activated, t + 1 + 1)
                    for k in range(KT1):
                        last = nc.tensor.transpose(psum_out[:, k * P:(k + 1) * P],
                                                   z_act[:, k * P:(k + 1) * P], ident[:, :])
                    last.then_inc(turned, 1)

                def tile(t, first=False, last=False):
                    for g in range(GROUPS):
                        if not (last and g == GROUPS - 1):
                            transpose(*following(t, g))
                        if g == 0 and not first:
                            pe.wait_ge(acc_copied, t)
                        if g == 1 and not first:
                            turn(t - 1)
                        multiply(t, g)

                pe.sem_inc(transposed, GROUPS)
                pe.sem_inc(multiplied, GROUPS)
                pe.sem_inc(turned, 1)
                transpose(0, 0)
                tile(0, first=True)
                with pe.Fori(1, TILES - 1) as t:
                    tile(t)
                tile(TILES - 1, last=True)
                turn(TILES - 1)


PLAN_STEPS_1 = 12
PLAN_STEPS_2 = 13


def kernel(**inputs):
    import concourse.bacc as bacc
    from concourse.bass_utils import run_bass_kernel_spmd as run

    a = {k.removeprefix("L0_conv_"): np.asarray(v) for k, v in inputs.items()}
    where, inside, shift = pixel_constants()
    arrays = {
        "x": a["x"].reshape(N_IMAGES, C_OUT, IMAGE),
        "w1": np.concatenate([a["w1"][:, :, 0, 0], a["w_off1"][:, :, 0, 0]]).T,
        "norm1": np.stack([a[n] for n in ("g1", "v1", "m1", "bb1", "b1")]),
        "w_off2": np.pad(a["w_off2"].transpose(2, 1, 3, 0), ((0, 0), (0, 0), (0, 0), (0, DX - 3 * TAPS)))
        .reshape(3, C_MID, 3 * DX),
        "w2": a["w2"].transpose(2, 3, 1, 0).reshape(TAPS * C_MID, C_OUT),
        "norm2": np.stack([a[n] for n in ("g2", "v2", "m2", "bb2", "b2")]),
        "b_off1": a["b_off1"].reshape(1, 3),
        "b_off2": a["b_off2"].reshape(1, 3 * TAPS),
        "where": where,
        "inside": inside,
        "shift": shift,
        "identity": np.eye(P, dtype=np.float32),
    }
    arrays = {k: np.ascontiguousarray(v) for k, v in arrays.items()}
    nc = bacc.Bacc("TRN2", target_bir_lowering=False, num_devices=1)
    args = [nc.dram_tensor(k, v.shape, mybir.dt.from_np(v.dtype), kind="ExternalInput").ap()
            for k, v in arrays.items()]
    out = nc.dram_tensor("out", (N_IMAGES, C_OUT, IMAGE), mybir.dt.float32, kind="ExternalOutput").ap()
    deformable_kernel(nc, *args, out)
    r = run(nc, [arrays], core_ids=[0])
    return r.results[0]["out"].reshape(N_IMAGES, C_OUT, HEIGHT, WIDTH)
```

```python
from contextlib import ExitStack

import numpy as np

import concourse.bass as bass
from concourse import mybir

N_IMAGES, C_OUT, HEIGHT, WIDTH = 8, 512, 52, 52
C_MID = C_OUT // 2
IMAGE = HEIGHT * WIDTH
P = 128
PIXELS = N_IMAGES * IMAGE
TILES = PIXELS // P
CHUNK = 13
CHUNKS = TILES // CHUNK
CHUNK_PX = CHUNK * P
TAPS = 9
GROUP = 3
GROUPS = TAPS // GROUP
TABLE_ROWS = PIXELS + WIDTH
EPS, SLOPE = 1e-5, 0.1
ROUND = 1.5 * 2.0**23
HALVES = ((0, 6), (6, 7))
QUARTERS = ((0, 3), (3, 3), (6, 3), (9, 4))
BLOCKS = ((0, 3), (3, 3), (6, 3), (9, 2), (11, 2))
DX = 32
SLOTS = 7
TAIL = 2 * P


def pixel_constants():
    g = np.arange(PIXELS)
    y, x, first = g % IMAGE // WIDTH, g % WIDTH, g // IMAGE * IMAGE + WIDTH
    where = np.zeros((TILES + 1, P, 3), np.float32)
    where[0, :, 2] = WIDTH
    where[1:] = np.stack([y, x, first], -1).reshape(TILES, P, 3)
    inside = np.zeros((TILES + 1, P, TAPS), np.float32)
    for k in range(TAPS):
        ty, tx = y + k // 3 - 1, x + k % 3 - 1
        inside[1:, :, k] = ((ty >= 0) & (ty < HEIGHT) & (tx >= 0) & (tx < WIDTH)).reshape(TILES, P)
    shift = np.array([[k // 3 - 1 for k in range(TAPS)] + [k % 3 - 1 for k in range(TAPS)]], np.float32)
    return where.transpose(1, 0, 2).copy(), inside.transpose(1, 0, 2).copy(), shift


def pieces(first, count):
    end = (first // IMAGE + 1) * IMAGE
    cut = end - first if first < end < first + count else count // 2
    return [((first + o) // IMAGE, (first + o) % IMAGE, o, n) for o, n in ((0, cut), (cut, count - cut))]


def deformable_kernel(nc, x, w1, norm1, w_off2, w2, norm2, norm2_col, b_off1, b_off2, where, inside, shift,
                      identity, out):
    f32, f32r = mybir.dt.float32, mybir.dt.float32r
    u32, u16 = mybir.dt.uint32, mybir.dt.uint16
    ALU, ACT, AX = mybir.AluOpType, mybir.ActivationFunctionType, mybir.AxisListType
    ds = bass.ds

    table1 = nc.dram_tensor("table1", [TABLE_ROWS, 2 * C_MID], f32, kind="Internal").ap()
    table2 = nc.dram_tensor("table2", [TABLE_ROWS, 2 * C_MID], f32, kind="Internal").ap()
    KT1 = C_OUT // P
    KT2 = C_MID // P
    N1 = C_MID + 4
    N_OFF = 3 * TAPS
    SLABS = TAPS * KT2
    NORMS = 5

    with ExitStack() as ctx:
        def sb(name, shape, dt=f32):
            return ctx.enter_context(nc.sbuf_tensor(name, shape, dt))

        def ps(name, cols):
            return ctx.enter_context(nc.psum_tensor(name, [P, cols], f32))

        def sem(name):
            return ctx.enter_context(nc.semaphore(name))

        w2_hi = sb("w2_hi", [P, SLABS, C_OUT], f32r)
        w2_lo = sb("w2_lo", [P, SLABS, C_OUT], f32r)
        val_hi = sb("val_hi", [P, GROUPS, GROUP * C_MID], f32r)
        val_lo = sb("val_lo", [P, GROUPS, GROUP * C_MID], f32r)
        norm2_cols = sb("norm2_cols", [P, NORMS, KT1])
        bias2 = sb("bias2", [P, KT1])
        ident = sb("ident", [P, P])
        boff1 = sb("boff1", [P, 3])
        boff2 = sb("boff2", [P, N_OFF])
        shifts = sb("shifts", [P, 2 * TAPS])
        row_cur = sb("row_cur", [P, 16], u32)

        area_a = sb("area_a", [P, KT1 * CHUNK_PX + KT1 * N1])
        x_sb = area_a[:, 0:KT1 * CHUNK_PX].rearrange("p (k n) -> p k n", k=KT1)
        w1_sb = area_a[:, KT1 * CHUNK_PX:].rearrange("p (k n) -> p k n", k=KT1)
        HT = TAIL + CHUNK_PX + 64
        h_stage = area_a[:, 0:CHUNK * C_MID].rearrange("p (t c) -> p t c", t=CHUNK)
        h_t = area_a[:, CHUNK * C_MID:CHUNK * C_MID + KT2 * HT].rearrange("p (k n) -> p k n", k=KT2)
        stage = x_sb
        area_b = sb("area_b", [P, SLOTS * 4 * C_MID + (TILES + 1) * TAPS + 9 * P])
        HALF_SLABS = SLABS // 2
        w2_raw = area_b[:, 0:HALF_SLABS * C_OUT].rearrange("p (s n) -> p s n", s=HALF_SLABS)
        at = HALF_SLABS * C_OUT
        norm1_sb = area_b[:, at:at + NORMS * C_MID].rearrange("p (v n) -> p v n", v=NORMS)
        at += NORMS * C_MID
        norm2_sb = area_b[:, at:at + NORMS * C_OUT].rearrange("p (v n) -> p v n", v=NORMS)
        gather1 = area_b[:, 0:SLOTS * 4 * C_MID].rearrange("p (s q c) -> p s q c", s=SLOTS, q=4)
        at = SLOTS * 4 * C_MID
        inside_sb = area_b[:, at:at + (TILES + 1) * TAPS].rearrange("p (t k) -> p t k", k=TAPS)
        at += (TILES + 1) * TAPS
        q_sb = area_b[0:3 * DX, at:at + 9 * P].rearrange("p (y n) -> p y n", y=3)
        gather2 = area_b[:, 0:TAPS * 4 * C_MID].rearrange("p (s q c) -> p s q c", s=TAPS, q=4)
        X_SLOTS = 4
        x_hi, x_lo = (v[:, :, :].rearrange("p g n -> p (g n)")[:, 0:X_SLOTS * C_OUT]
                      .rearrange("p (s k n) -> p s k n", s=X_SLOTS, k=KT1) for v in (val_hi, val_lo))
        C_SIZE = 4326
        area_c = sb("area_c", [P, C_SIZE])
        at = 0

        def part(n):
            nonlocal at
            at += n
            assert at <= C_SIZE, at
            return area_c[:, at - n:at]

        woff_sb = part(KT2 * TAPS * DX).rearrange("p (k y n) -> p k y n", k=KT2, y=3)
        weights1 = part(4 * TILES).rearrange("p (q t) -> p q t", q=4)
        index1 = part(TILES)
        bias1 = part(C_MID)
        where_sb = part((TILES + 1) * 3).rearrange("p (t v) -> p t v", v=3)
        om = part(CHUNK * N_OFF).rearrange("p (t n) -> p t n", t=CHUNK)
        spot = part(CHUNK * 2 * TAPS)
        corner = part(CHUNK * 2 * TAPS)
        near = part(CHUNK * 2 * TAPS)
        far = part(CHUNK * 2 * TAPS)
        gate = part(CHUNK * TAPS)
        prod = part(3 * TAPS * N_OFF)
        offsets1 = prod[:, 0:TILES * 3].rearrange("p (t v) -> p t v", t=TILES)
        at = 0
        val = part(TAPS * C_MID).rearrange("p (g k c) -> p g k c", g=GROUPS, k=GROUP)
        val_too = part(GROUPS * C_MID).rearrange("p (g c) -> p g c", g=GROUPS)
        acc_sb = part(C_OUT)
        z_sb = part(C_OUT).rearrange("p (k n) -> p k n", k=KT1)

        psum_t = ps("psum_t", 8 * 512)
        psum_acc = psum_t[:, 6 * 512:7 * 512]
        psum_out = psum_t[:, 7 * 512:]

        gather_cleared = sem("gather_cleared")

        def group_t(g):
            return psum_t[:, 1024 * g:1024 * g + GROUP * C_MID]

        def offsets_of(tiles, k):
            return om.rearrange("p t n -> p (t n)")[:, 0:tiles * 3 * k].rearrange("p (t n) -> p t n", t=tiles)

        def sample_plan(dve, link, gate_ready, om_ready, tiles, k, raw, slot, base, wts, rows,
                        gate_count):
            n = tiles * 2 * k
            o = offsets_of(tiles, k)

            def two(t):
                return t[:, 0:n].rearrange("p (t v) -> p t v", t=tiles)

            def axis(t, a):
                return two(t)[:, :, a * k:(a + 1) * k]

            b_off = (boff1 if k == 1 else boff2)[:, 0:3 * k]
            yx = where_sb[:, ds(slot, tiles), 0:2]
            first = where_sb[:, ds(slot, tiles), 2:3]
            m = gate[:, 0:tiles * k].rearrange("p (t k) -> p t k", k=k)
            nc.vector.tensor_tensor(o, raw, b_off.unsqueeze(1).to_broadcast([P, tiles, 3 * k]), ALU.add)\
                .then_inc(om_ready, 1)
            dve.wait_ge(om_ready, gate_count + 1)
            if k == 1:
                link(nc.vector.tensor_tensor(two(spot), o[:, :, 0:2], yx, ALU.add))
            else:
                for a in range(2):
                    last = nc.vector.tensor_tensor(
                        axis(spot, a), yx[:, :, a:a + 1].to_broadcast([P, tiles, k]),
                        shifts[:, a * k:(a + 1) * k].unsqueeze(1).to_broadcast([P, tiles, k]), ALU.add)
                link(last)
                link(nc.vector.tensor_tensor(two(spot), o[:, :, 0:2 * k], two(spot), ALU.add))
            link(nc.vector.tensor_scalar(two(corner), two(spot), 0.0, float(HEIGHT - 1), ALU.max, ALU.min))
            link(nc.vector.tensor_scalar(two(corner), two(corner), -0.5, ROUND, ALU.add, ALU.add))
            link(nc.vector.tensor_scalar(two(corner), two(corner), ROUND, None, ALU.subtract))
            link(nc.vector.tensor_tensor(two(spot), two(spot), two(corner), ALU.subtract))
            link(nc.vector.tensor_scalar(two(near), two(spot), -1.0, 1.0, ALU.mult, ALU.add))
            link(nc.vector.scalar_tensor_tensor(out=two(near), in0=two(spot), scalar=1.0, in1=two(near),
                                                op0=ALU.add, op1=ALU.min))
            link(nc.vector.tensor_scalar(two(far), two(spot), -1.0, 2.0, ALU.mult, ALU.add))
            link(nc.vector.scalar_tensor_tensor(out=two(far), in0=two(far), scalar=0.0, in1=two(spot),
                                                op0=ALU.max, op1=ALU.min))
            dve.wait_ge(gate_ready, gate_count)
            for t in (near, far):
                last = nc.vector.scalar_tensor_tensor(out=axis(t, 0), in0=axis(t, 0), scalar=0.0, in1=m,
                                                      op0=ALU.max, op1=ALU.mult)
            link(last)
            for q, (ty, tx) in enumerate(((near, near), (far, near), (near, far), (far, far))):
                nc.vector.scalar_tensor_tensor(
                    out=wts[:, q, base].rearrange("p (t k) -> p t k", k=k), in0=axis(tx, 1), scalar=0.0,
                    in1=axis(ty, 0), op0=ALU.max, op1=ALU.mult)
            link(nc.vector.scalar_tensor_tensor(out=axis(spot, 0), in0=axis(corner, 0), scalar=float(WIDTH),
                                                in1=axis(corner, 1), op0=ALU.mult, op1=ALU.add))
            link(nc.vector.tensor_tensor(rows[:, base].rearrange("p (t k) -> p t k", k=k), axis(spot, 0),
                                         first.to_broadcast([P, tiles, k]), ALU.add))

        def linker(dve, done):
            count = [0]

            def link(ins):
                count[0] += 1
                ins.then_inc(done, 1)
                dve.wait_ge(done, count[0])
            return link, count

        def table_writes(eng, table, source, c, half, written):
            j, n = HALVES[half]
            for row, col in ((WIDTH, 0), (0, C_MID)):
                dst = table[ds(c * CHUNK_PX + row + j * P, n * P), col:col + C_MID]
                eng.dma_start(dst.rearrange("(t p) c -> p t c", p=P), source[:, j:j + n, 0:C_MID])\
                    .then_inc(written, 16)

        with ExitStack() as phase:
            def sem(name):
                return phase.enter_context(nc.semaphore(name))

            y_stage = phase.enter_context(nc.sbuf_tensor("y_stage", [P, CHUNK, C_MID], f32))
            w1_hi = phase.enter_context(nc.sbuf_tensor("w1_hi", [P, KT1, N1], f32r))
            w1_lo = phase.enter_context(nc.sbuf_tensor("w1_lo", [P, KT1, N1], f32r))
            first_loaded = sem("first_loaded")
            const_loaded = sem("const_loaded")
            x_loaded = [sem(f"x_loaded_{q}") for q in range(4)]
            raw_loaded = [sem("raw_loaded_a"), sem("raw_loaded_b")]
            hi_ready = sem("x_hi_ready")
            x_split = sem("x_split")
            x_used = sem("x_used")
            y_copied = sem("y_copied")
            table_written = [sem("table_written_a"), sem("table_written_b")]
            root_ready = sem("root_ready")
            var_ready = sem("var_ready")
            edge_cleared = sem("edge_cleared")
            edge_written = sem("edge_written")
            w1_scaled = sem("w1_scaled")
            w2_split = sem("w2_split")
            om_ready = sem("om_ready")
            gate_ready = sem("gate_ready")
            chain = sem("chain")
            setup = sem("setup")
            block = phase.enter_context(nc.Block())
            CONSTS = 9
            PLANS = ((0, CHUNK * TAPS), (CHUNK * TAPS, TILES - CHUNK * TAPS))

            X_SLOT = [j % X_SLOTS for j in range(CHUNK - 1)] + [2]
            X_BACK = [next(b for b in range(1, CHUNK) if X_SLOT[(j - b) % CHUNK] == X_SLOT[j])
                      for j in range(CHUNK)]
            MOST_BACK = max(X_BACK)

            def x_tile(j):
                return x_sb[:, :, j * P:(j + 1) * P]

            def y_bank(j):
                b = j % 7
                return psum_acc[:, 0:N1] if b == 6 else psum_t[:, 512 * b:512 * b + N1]

            @block.sync
            def _(sp):
                sp.dma_start(w1_sb, w1.rearrange("(k p) n -> p k n", p=P)).then_inc(first_loaded, 16)
                sp.dma_start(norm1_sb, norm1.unsqueeze(0).to_broadcast([P, NORMS, C_MID]))\
                    .then_inc(first_loaded, 16)
                for c in range(CHUNKS):
                    for quarter, (j, n) in enumerate(QUARTERS):
                        if c:
                            sp.wait_ge(x_split, CHUNK * (c - 1) + j + n)
                        for image, px, o, count in pieces(c * CHUNK_PX + j * P, n * P):
                            sp.dma_start(x_sb[:, :, j * P + o:j * P + o + count],
                                         x[image].rearrange("(k p) n -> p k n", p=P)[:, :, px:px + count])\
                                .then_inc(x_loaded[quarter], 16)
                        if c == 0 and quarter == 0:
                            for dst, src in (
                                (norm2_sb, norm2.unsqueeze(0).to_broadcast([P, NORMS, C_OUT])),
                                (norm2_cols[:, :, :], norm2_col),
                                (boff1[:, :], b_off1.to_broadcast([P, 3])),
                                (boff2[:, :], b_off2.to_broadcast([P, N_OFF])),
                                (shifts[:, :], shift.to_broadcast([P, 2 * TAPS])),
                                (ident[:, :], identity),
                                (where_sb, where),
                            ):
                                sp.dma_start(dst, src).then_inc(const_loaded, 16)
                            for k in range(KT2):
                                sp.dma_start(woff_sb[:, k, :, :],
                                             w_off2[:, k * P:(k + 1) * P, :].rearrange("y p n -> p y n"))\
                                    .then_inc(const_loaded, 16)

            @block.gpsimd
            def _(pool):
                nc.gpsimd.memset(prod[:, 0:C_MID], 0.0).then_inc(edge_cleared, 1)
                pool.wait_ge(edge_cleared, 1)
                for table in (table1, table2):
                    for row, col in ((0, 0), (PIXELS, C_MID)):
                        pool.dma_start(table[row:row + WIDTH, col:col + C_MID], prod[0:WIDTH, 0:C_MID])\
                            .then_inc(edge_written, 16)
                pool.wait_ge(w1_scaled, 1)
                for part_no in range(2):
                    if part_no:
                        pool.wait_ge(w2_split, HALF_SLABS)
                    pool.dma_start(w2_raw, w2[part_no * HALF_SLABS * P:(part_no + 1) * HALF_SLABS * P, :]
                                   .rearrange("(s p) n -> p s n", p=P)).then_inc(raw_loaded[part_no], 16)
                pool.wait_ge(edge_written, 64)

            @block.tensor
            def _(pe):
                pe.sem_inc(x_used, MOST_BACK)
                pe.wait_ge(w1_scaled, 1)
                with pe.Fori(0, CHUNKS) as c:
                    for j in range(CHUNK):
                        pe.wait_ge(x_split, c * CHUNK + j + 1)
                        pe.wait_ge(y_copied, c * CHUNK + j + 1)
                        for k in range(KT1):
                            for a, b in ((x_hi, w1_hi), (x_hi, w1_lo), (x_lo, w1_hi)):
                                last = nc.tensor.matmul(
                                    y_bank(j), a[:, X_SLOT[j], k, :], b[:, k, :],
                                    start=(k == 0 and a is x_hi and b is w1_hi),
                                    stop=(k == KT1 - 1 and a is x_lo))
                        last.then_inc(x_used, 1)

            @block.scalar
            def _(act):
                def root(norm, nth):
                    act.wait_ge(var_ready, nth)
                    nc.scalar.activation(norm[:, 1, :], norm[:, 1, :], ACT.Sqrt).then_inc(root_ready, 1)

                def upper(c, j):
                    for quarter, (j0, _) in enumerate(QUARTERS):
                        if j == j0:
                            act.wait_ge(x_loaded[quarter], (c + 1) * 32)
                    act.wait_ge(x_used, c * CHUNK + j + 1 - X_BACK[j] + MOST_BACK)
                    nc.scalar.activation(x_hi[:, X_SLOT[j], :, :], x_tile(j), ACT.Identity)\
                        .then_inc(hi_ready, 1)

                def copy_y(c, j):
                    for half, (j0, n) in enumerate(HALVES):
                        if j == j0:
                            act.wait_ge(table_written[half], (c + 1) * 32)
                    act.wait_ge(x_used, c * CHUNK + j + 1 + MOST_BACK)
                    nc.scalar.activation(y_stage[:, j, :], y_bank(j)[:, 0:C_MID], ACT.Copy)
                    nc.scalar.activation(offsets1[:, ds(c * CHUNK + j, 1), :],
                                         y_bank(j)[:, C_MID:C_MID + 3].unsqueeze(1), ACT.Copy).then_inc(y_copied, 1)
                    for half, (j0, n) in enumerate(HALVES):
                        if j == j0 + n - 1:
                            act.wait_ge(y_copied, c * CHUNK + 6 + j0 + n)
                            table_writes(act, table1, y_stage, c, half, table_written[half])

                def modulation(nth):
                    n = PLANS[nth][1]
                    act.wait_ge(om_ready, nth + 2)
                    nc.scalar.activation(gate[:, 0:n].unsqueeze(2), offsets_of(n, 1)[:, :, 2:3], ACT.Sigmoid)\
                        .then_inc(gate_ready, 1)

                def chunk(c, first=False, last=False):
                    for j in range(CHUNK):
                        upper(c, j)
                        if j >= 2:
                            copy_y(c, j - 2)
                        elif not first:
                            copy_y(c - 1, CHUNK - 2 + j)
                        if first and j == 3:
                            root(norm2_sb, 2)
                            root(norm2_cols, 3)
                        if last and j == 6:
                            modulation(0)

                root(norm1_sb, 1)
                act.sem_inc(y_copied, 6)
                for half in range(2):
                    act.sem_inc(table_written[half], 32)
                act.wait_ge(edge_written, 64)
                chunk(0, first=True)
                with act.Fori(1, CHUNKS - 1) as c:
                    chunk(c)
                chunk(CHUNKS - 1, last=True)
                for j in (CHUNK - 2, CHUNK - 1):
                    copy_y(CHUNKS - 1, j)
                modulation(1)
                for half in range(2):
                    act.wait_ge(table_written[half], (CHUNKS + 1) * 32)

            @block.vector
            def _(dve):
                link, count = linker(dve, setup)

                def fold(norm, bias=None):
                    link(nc.vector.reciprocal(norm[:, 1, :], norm[:, 1, :]))
                    link(nc.vector.tensor_tensor(norm[:, 0, :], norm[:, 0, :], norm[:, 1, :], ALU.mult))
                    if bias is None:
                        return
                    link(nc.vector.tensor_tensor(bias, norm[:, 4, :], norm[:, 2, :], ALU.subtract))
                    link(nc.vector.tensor_tensor(bias, bias, norm[:, 0, :], ALU.mult))
                    link(nc.vector.tensor_tensor(bias, bias, norm[:, 3, :], ALU.add))


                def variance(norm):
                    nc.vector.tensor_scalar(norm[:, 1, :], norm[:, 1, :], EPS, None, ALU.add)\
                        .then_inc(var_ready, 1)

                dve.sem_inc(om_ready, 1)
                dve.wait_ge(first_loaded, 32)
                variance(norm1_sb)
                dve.wait_ge(root_ready, 1)
                fold(norm1_sb, bias1)
                for k in range(KT1):
                    last = nc.vector.tensor_tensor(w1_sb[:, k, 0:C_MID], w1_sb[:, k, 0:C_MID],
                                                   norm1_sb[:, 0, :], ALU.mult)
                link(last)
                link(nc.vector.tensor_copy(w1_hi[:, :, :], w1_sb))
                nc.vector.tensor_tensor(w1_lo[:, :, :], w1_sb, w1_hi[:, :, :].bitcast(f32), ALU.subtract).then_inc(w1_scaled, 1)

                def fold_norm2():
                    dve.wait_ge(const_loaded, 16 * CONSTS)
                    variance(norm2_sb)
                    variance(norm2_cols)
                    dve.wait_ge(root_ready, 3)
                    fold(norm2_sb)
                    fold(norm2_cols, bias2[:, :])

                def split_w2(slab):
                    part_no, s = divmod(slab, HALF_SLABS)
                    if s == 0:
                        dve.wait_ge(raw_loaded[part_no], 16)
                    hi, lo = w2_hi[:, slab, :], w2_lo[:, slab, :]
                    link(nc.vector.tensor_tensor(w2_raw[:, s, :], w2_raw[:, s, :], norm2_sb[:, 0, :],
                                                 ALU.mult))
                    link(nc.vector.tensor_copy(hi, w2_raw[:, s, :]))
                    nc.vector.tensor_tensor(lo, w2_raw[:, s, :], hi.bitcast(f32), ALU.subtract)\
                        .then_inc(w2_split, 1)

                def lower(c, j):
                    dve.wait_ge(hi_ready, c * CHUNK + j + 1)
                    nc.vector.tensor_tensor(x_lo[:, X_SLOT[j], :, :], x_tile(j),
                                            x_hi[:, X_SLOT[j], :, :].bitcast(f32), ALU.subtract)\
                        .then_inc(x_split, 1)

                def plan(nth):
                    tile0, n = PLANS[nth]
                    dve.wait_ge(y_copied, tile0 + n + 6)
                    steps = [0]

                    def link_in_plan(ins):
                        steps[0] += 1
                        ins.then_inc(chain, 1)
                        dve.wait_ge(chain, nth * PLAN_STEPS_1 + steps[0])

                    sample_plan(dve, link_in_plan, gate_ready, om_ready, n, 1, offsets1[:, tile0:tile0 + n, :],
                                tile0 + 1, ds(tile0, n), weights1, index1, nth + 1)
                    assert steps[0] == PLAN_STEPS_1, steps

                def chunk(c, first=False, last=False, slabs=()):
                    slabs = list(slabs)
                    for j in range(CHUNK):
                        lower(c, j)
                        if first and j == 3:
                            fold_norm2()
                        if last and j == 5:
                            plan(0)
                        if slabs and j % 2 == 0 and not (first and j < 6):
                            split_w2(slabs.pop(0))
                    assert not slabs

                chunk(0, first=True, slabs=range(0, 4))
                chunk(1, slabs=range(4, 9))
                chunk(2, slabs=range(9, 16))
                chunk(3, slabs=range(16, 18))
                with dve.Fori(4, CHUNKS - 1) as c:
                    chunk(c)
                chunk(CHUNKS - 1, last=True)
                plan(1)

        weights2 = sb("weights2", [P, 4, (TILES + 1) * TAPS])
        index2 = sb("index2", [P, (TILES + 1) * TAPS], u16)

        with ExitStack() as phase:
            def sem(name):
                return phase.enter_context(nc.semaphore(name))

            inside_loaded = sem("inside_loaded")
            h_t_cleared = sem("h_t_cleared")
            rows_copied = sem("rows_copied")
            gathered = [sem(f"gathered1_{s}") for s in range(SLOTS)]
            sampled = sem("sampled")
            summed = sem("summed")
            h_ready = sem("h_ready")
            h_transposed = sem("h_transposed")
            h_t_ready = sem("h_t_ready")
            tail_kept = sem("tail_kept")
            convolved = sem("convolved")
            conv_copied = sem("conv_copied")
            conv_turned = sem("conv_turned")
            masked = sem("masked")
            reduced = sem("reduced")
            table_written = [sem("table2_written_a"), sem("table2_written_b")]
            om_ready = sem("om2_ready")
            gate_ready = sem("gate2_ready")
            chain = sem("chain2")
            block = phase.enter_context(nc.Block())
            LAST_BLOCK = len(BLOCKS) - 1
            FINAL = (0, 1)

            def t_bank(j):
                b = 512 * (j % 3 if j < CHUNK - 2 else j - (CHUNK - 2))
                return psum_t[:, b:b + C_MID]

            def conv_bank(u, n):
                b = 512 * (3 + u % 2)
                return psum_t[0:3 * DX, b:b + n * P + 2]

            def off_bank(i):
                return off_banks[:, i, :]

            off_banks = psum_t[:, 512 * 5:].rearrange("p (t n) -> p t n", t=3)

            @block.sync
            def _(sp):
                sp.dma_start(inside_sb, inside).then_inc(inside_loaded, 16)
                sp.wait_ge(inside_loaded, 16)

            @block.gpsimd
            def _(pool):
                with pool.Fori(0, CHUNKS) as c:
                    for half, (j0, n) in enumerate(HALVES):
                        pool.wait_ge(sampled, c * CHUNK + j0 + n)
                        nc.gpsimd.tensor_copy(row_cur[:, j0:j0 + n], index1[:, ds(c * CHUNK + j0, n)])\
                            .then_inc(rows_copied, 1)
                        pool.wait_ge(rows_copied, 2 * c + half + 1)
                        for j in range(j0, j0 + n):
                            back = SLOTS if j >= SLOTS else CHUNK if j + SLOTS >= CHUNK else CHUNK - SLOTS
                            pool.wait_ge(sampled, c * CHUNK + j + 1 - back + CHUNK)
                            pool.sem_inc(gather_cleared, 1)
                            nc.gpsimd.indirect_dma_start(
                                gather1[:, j % SLOTS, :, :].rearrange("p q c -> p (q c)"), None,
                                table1, bass.IndirectOffsetOnAxis(ap=row_cur[:, j:j + 1], axis=0))\
                                .then_inc(gathered[j % SLOTS], 16)

            @block.tensor
            def _(pe):
                def transpose_h(c, b):
                    j0, n = BLOCKS[b]
                    for j in range(j0, j0 + n):
                        pe.wait_ge(h_ready, c * CHUNK + j + 1)
                        pe.wait_ge(h_t_ready, c * CHUNK + j + 1)
                        for kt in range(KT2):
                            last = nc.tensor.transpose(t_bank(j)[:, kt * P:(kt + 1) * P],
                                                       h_stage[:, j, kt * P:(kt + 1) * P], ident[:, :])
                        last.then_inc(h_transposed, 1)

                def convolve(c, b, block):
                    j0, n = block
                    for y in range(3):
                        u = 3 * b + y
                        pe.wait_ge(conv_copied, c * 3 * len(BLOCKS) + u + (1 if u else 2))
                        at = TAIL + (j0 - 1) * P - 1 + (y - 1) * WIDTH
                        for kt in range(KT2):
                            last = nc.tensor.matmul(conv_bank(u, n), woff_sb[:, kt, y, :],
                                                    h_t[:, kt, at:at + n * P + 2],
                                                    start=(kt == 0), stop=(kt == KT2 - 1))
                        last.then_inc(convolved, 1)

                def turn_conv(c, b, block):
                    j0, n = block
                    pe.wait_ge(conv_copied, (c * len(BLOCKS) + b + 1) * 3 + 2)
                    pe.wait_ge(masked, c * len(BLOCKS) + b + 1)
                    for i in range(n):
                        for y in range(3):
                            last = nc.tensor.transpose(off_bank(i)[:, y * 3 * DX:(y + 1) * 3 * DX],
                                                       q_sb[:, y, i * P:(i + 1) * P],
                                                       ident[0:3 * DX, 0:3 * DX])
                    last.then_inc(conv_turned, 1)

                def chunk(c, first=False):
                    for b, blk in enumerate(BLOCKS):
                        transpose_h(c, b)
                        if b:
                            turn_conv(c, b - 1, BLOCKS[b - 1])
                        elif not first:
                            turn_conv(c - 1, LAST_BLOCK, BLOCKS[LAST_BLOCK])
                        j0, n = blk
                        pe.wait_ge(h_t_ready, c * CHUNK + j0 + n + 2)
                        if b == 0:
                            pe.wait_ge(tail_kept, c + 1)
                        convolve(c, b, blk)

                chunk(0, first=True)
                with pe.Fori(1, CHUNKS) as c:
                    chunk(c)
                turn_conv(CHUNKS - 1, LAST_BLOCK, BLOCKS[LAST_BLOCK])
                pe.wait_ge(tail_kept, CHUNKS + 1)
                convolve(CHUNKS, 0, FINAL)
                turn_conv(CHUNKS, 0, FINAL)

            @block.scalar
            def _(act):
                act.sem_inc(h_t_ready, 2)
                act.sem_inc(conv_copied, 2)
                for half in range(2):
                    act.sem_inc(table_written[half], 32)
                act.wait_ge(h_t_cleared, 1)
                act.sem_inc(tail_kept, 1)

                def copy_h_t(c, b):
                    j0, n = BLOCKS[b]
                    for j in range(j0, j0 + n):
                        act.wait_ge(h_transposed, c * CHUNK + j + 1)
                        nc.scalar.activation(h_t[:, :, TAIL + j * P:TAIL + (j + 1) * P],
                                             t_bank(j).rearrange("p (k n) -> p k n", k=KT2),
                                             ACT.Copy).then_inc(h_t_ready, 1)

                def copy_conv(c, b, block):
                    j0, n = block
                    act.wait_ge(conv_turned, c * len(BLOCKS) + b + 1)
                    for y in range(3):
                        act.wait_ge(convolved, (c * len(BLOCKS) + b) * 3 + y + 1)
                        for dx in range(3):
                            rows = slice(dx * DX, (dx + 1) * DX)
                            last = nc.scalar.activation(q_sb[rows, y, 0:n * P],
                                                        conv_bank(3 * b + y, n)[rows, dx:dx + n * P],
                                                        ACT.Copy)
                        last.then_inc(conv_copied, 1)

                def modulation(count, tiles):
                    act.wait_ge(om_ready, count)
                    nc.scalar.activation(gate[:, 0:tiles * TAPS].rearrange("p (t k) -> p t k", k=TAPS),
                                         om[:, 0:tiles, 2 * TAPS:], ACT.Sigmoid).then_inc(gate_ready, 1)

                def chunk(c, first=False):
                    for b, blk in enumerate(BLOCKS):
                        copy_h_t(c, b)
                        if b == 1 and not first:
                            modulation(c + 1, CHUNK)
                        copy_conv(c, b, blk)
                        for half, (j0, n) in enumerate(HALVES):
                            if blk[0] + blk[1] == j0 + n:
                                act.wait_ge(h_ready, c * CHUNK + j0 + n)
                                table_writes(act, table2, h_stage, c, half, table_written[half])
                    act.wait_ge(h_t_ready, (c + 1) * CHUNK + 2)
                    nc.scalar.activation(h_t[:, :, 0:TAIL], h_t[:, :, CHUNK_PX:CHUNK_PX + TAIL],
                                         ACT.Copy).then_inc(tail_kept, 1)

                chunk(0, first=True)
                with act.Fori(1, CHUNKS) as c:
                    chunk(c)
                modulation(CHUNKS + 1, CHUNK)
                copy_conv(CHUNKS, 0, FINAL)
                act.wait_ge(gate_ready, CHUNKS)
                modulation(CHUNKS + 2, 1)
                for half in range(2):
                    act.wait_ge(table_written[half], (CHUNKS + 1) * 32)

            @block.vector
            def _(dve):
                nc.vector.memset(h_t, 0.0).then_inc(h_t_cleared, 1)
                dve.sem_inc(sampled, CHUNK)
                dve.sem_inc(masked, 1)
                dve.sem_inc(reduced, 1)
                dve.sem_inc(om_ready, 1)
                dve.sem_inc(conv_turned, 1)
                dve.wait_ge(inside_loaded, 16)
                dve.wait_ge(h_t_cleared, 1)

                def sample_h(c, b):
                    j0, n = BLOCKS[b]
                    for half in range(2):
                        if j0 == HALVES[half][0]:
                            dve.wait_ge(table_written[half], (c + 1) * 32)
                    for q in range(4):
                        for j in range(j0, j0 + n):
                            nth = c * CHUNK + j
                            if q == 0:
                                uses = 2 if j + SLOTS < CHUNK or j >= SLOTS else 1
                                dve.wait_ge(gathered[j % SLOTS], (c * uses + (1 if j >= SLOTS else 0) + 1) * 16)
                            else:
                                dve.wait_ge(summed, 3 * (c * CHUNK + j0) + (q - 1) * n + j - j0 + 1)
                            v = h_stage[:, j, :]
                            ins = nc.vector.scalar_tensor_tensor(
                                out=v, in0=gather1[:, j % SLOTS, q, :], scalar=weights1[:, q, ds(nth, 1)],
                                in1=bias1 if q == 0 else v, op0=ALU.mult, op1=ALU.add)
                            ins.then_inc(sampled if q == 3 else summed, 1)
                    for j in range(j0, j0 + n):
                        dve.wait_ge(sampled, c * CHUNK + j + 1 + CHUNK)
                        v = h_stage[:, j, :]
                        nc.vector.scalar_tensor_tensor(out=v, in0=v, scalar=SLOPE, in1=v, op0=ALU.mult,
                                                       op1=ALU.max).then_inc(h_ready, 1)

                def offsets(c, b, block):
                    j0, n = block
                    nth = c * len(BLOCKS) + b
                    dve.wait_ge(conv_turned, nth + 2)
                    dve.wait_ge(reduced, nth + 1)
                    nc.vector.tensor_tensor(
                        prod[:, 0:n * TAPS * N_OFF].rearrange("p (t k n) -> p t k n", t=n, k=TAPS),
                        off_banks[:, 0:n, 0:TAPS * DX].rearrange("p t (k n) -> p t k n", k=TAPS)[:, :, :, 0:N_OFF],
                        inside_sb[:, ds(c * CHUNK + j0, n), :].unsqueeze(3).to_broadcast([P, n, TAPS, N_OFF]),
                        ALU.mult).then_inc(masked, 1)
                    dve.wait_ge(masked, nth + 2)
                    nc.vector.tensor_reduce(
                        om[:, j0:j0 + n, :],
                        prod[:, 0:n * TAPS * N_OFF].rearrange("p (t k n) -> p t n k", t=n, k=TAPS),
                        AX.X, ALU.add).then_inc(reduced, 1)

                def plan_chunk(c, tiles, base):
                    dve.wait_ge(reduced, (c * len(BLOCKS) + (len(BLOCKS) if tiles > 1 else 1)) + 1)
                    steps = [0]

                    def link_in_chunk(ins):
                        steps[0] += 1
                        ins.then_inc(chain, 1)
                        dve.wait_ge(chain, c * PLAN_STEPS_2 + steps[0])

                    sample_plan(dve, link_in_chunk, gate_ready, om_ready, tiles, TAPS, om[:, 0:tiles, :],
                                c * CHUNK, base, weights2, index2, c + 1)
                    assert steps[0] == PLAN_STEPS_2, steps

                def chunk(c, first=False):
                    for b, blk in enumerate(BLOCKS):
                        sample_h(c, b)
                        if b >= 2:
                            offsets(c, b - 2, BLOCKS[b - 2])
                        elif not first:
                            offsets(c - 1, b - 2 + len(BLOCKS), BLOCKS[b - 2])
                            if b == 1:
                                plan_chunk(c - 1, CHUNK, ds((c - 1) * CHUNK * TAPS, CHUNK * TAPS))

                chunk(0, first=True)
                with dve.Fori(1, CHUNKS) as c:
                    chunk(c)
                for b in (LAST_BLOCK - 1, LAST_BLOCK):
                    offsets(CHUNKS - 1, b, BLOCKS[b])
                plan_chunk(CHUNKS - 1, CHUNK, ds((CHUNKS - 1) * CHUNK * TAPS, CHUNK * TAPS))
                offsets(CHUNKS, 0, FINAL)
                plan_chunk(CHUNKS, 1, ds(CHUNKS * CHUNK * TAPS, TAPS))

        with ExitStack() as phase:
            def sem(name):
                return phase.enter_context(nc.semaphore(name))

            x_loaded = [sem(f"residual_loaded_{q}") for q in range(4)]
            stored = [sem(f"stored_{q}") for q in range(4)]
            rows_copied = sem("rows_copied3")
            gathered = [sem(f"gathered3_{g}") for g in range(GROUPS)]
            scaled = sem("scaled")
            summed = sem("summed3")
            sampled = sem("sampled3")
            transposed = sem("transposed")
            hi_ready = sem("hi_ready")
            lo_ready = sem("lo_ready")
            multiplied = sem("multiplied")
            acc_copied = sem("acc_copied")
            turned = sem("turned")
            biased = sem("biased")
            activated = sem("activated")
            finished = sem("finished")
            block = phase.enter_context(nc.Block())

            @block.sync
            def _(sp):
                def load(c, quarter):
                    j, n = QUARTERS[quarter]
                    for image, px, o, count in pieces(c * CHUNK_PX + j * P, n * P):
                        sp.dma_start(stage[:, :, j * P + o:j * P + o + count],
                                     x[image].rearrange("(k p) n -> p k n", p=P)[:, :, px:px + count])\
                            .then_inc(x_loaded[quarter], 16)

                sp.wait_ge(sampled, GROUPS + GROUPS)
                for quarter in range(4):
                    load(0, quarter)
                for c in range(CHUNKS):
                    for quarter, (j, n) in enumerate(QUARTERS):
                        sp.wait_ge(finished, c * CHUNK + j + n + 1)
                        for image, px, o, count in pieces(c * CHUNK_PX + j * P, n * P):
                            sp.dma_start(out[image].rearrange("(k p) n -> p k n", p=P)[:, :, px:px + count],
                                         stage[:, :, j * P + o:j * P + o + count])\
                                .then_inc(stored[quarter], 16)
                        sp.wait_ge(stored[quarter], (c + 1) * 32)
                        if c + 1 < CHUNKS:
                            load(c + 1, quarter)

            @block.gpsimd
            def _(pool):
                with pool.Fori(0, TILES) as t:
                    for g in range(GROUPS):
                        pool.wait_ge(sampled, t * GROUPS + g + 1)
                        nc.gpsimd.tensor_copy(row_cur[:, g * GROUP:(g + 1) * GROUP],
                                              index2[:, ds((t + 1) * TAPS + g * GROUP, GROUP)])\
                            .then_inc(rows_copied, 1)
                        pool.wait_ge(rows_copied, t * GROUPS + g + 1)
                        pool.sem_inc(gather_cleared, 1)
                        for k in range(g * GROUP, (g + 1) * GROUP):
                            nc.gpsimd.indirect_dma_start(
                                gather2[:, k, :, :].rearrange("p q c -> p (q c)"), None, table2,
                                bass.IndirectOffsetOnAxis(ap=row_cur[:, k:k + 1], axis=0))\
                                .then_inc(gathered[g], 16)

            def ahead(t, g, n):
                return t + (g + n) // GROUPS, (g + n) % GROUPS

            IN_PARTS = (2,)

            def weight(t, k, q):
                return weights2[:, q, ds((t + 1) * TAPS + k, 1)]

            @block.scalar
            def _(act):
                def scale(t, g):
                    act.wait_ge(gathered[g], (t + 1) * 16 * GROUP)
                    act.wait_ge(transposed, t * GROUPS + g + 1)
                    for k in range(GROUP):
                        last = nc.scalar.activation(val[:, g, k, :], gather2[:, g * GROUP + k, 0, :],
                                                    ACT.Identity, scale=weight(t, g * GROUP + k, 0))
                    if g in IN_PARTS:
                        last = nc.scalar.activation(val_too[:, g, :], gather2[:, g * GROUP + k, 1, :],
                                                    ACT.Identity, scale=weight(t, g * GROUP + k, 1))
                    last.then_inc(scaled, 1)

                def upper(t, g):
                    act.wait_ge(transposed, t * GROUPS + g + 1 + GROUPS)
                    act.wait_ge(multiplied, t * GROUPS + g + 1)
                    nc.scalar.activation(val_hi[:, g, :], group_t(g), ACT.Identity).then_inc(hi_ready, 1)

                def copy_acc(t):
                    act.wait_ge(multiplied, (t + 2) * GROUPS)
                    act.wait_ge(turned, t + 1)
                    nc.scalar.activation(acc_sb, psum_acc, ACT.Identity).then_inc(acc_copied, 1)

                def add_bias(t):
                    act.wait_ge(turned, t + 1 + 1)
                    act.wait_ge(finished, t + 1)
                    for k in range(KT1):
                        last = nc.scalar.activation(z_sb[:, k, :], psum_out[:, k * P:(k + 1) * P],
                                                    ACT.Identity, bias=bias2[:, k:k + 1])
                    last.then_inc(biased, 1)

                def tile(t, first=False, splits=GROUPS, scales=GROUPS):
                    for g in range(GROUPS):
                        if g < splits:
                            upper(*ahead(t, g, 2))
                        if g == 1 and not first:
                            add_bias(t - 1)
                        if g < scales:
                            scale(*ahead(t, g, 4))
                    copy_acc(t)

                act.sem_inc(biased, 1)
                for g in range(GROUPS):
                    scale(0, g)
                upper(0, 0)
                upper(0, 1)
                scale(1, 0)
                tile(0, first=True)
                with act.Fori(1, TILES - 2) as t:
                    tile(t)
                tile(TILES - 2, scales=GROUPS - 1)
                tile(TILES - 1, splits=GROUPS - 2, scales=0)
                add_bias(TILES - 1)

            @block.vector
            def _(dve):
                TWO_PARTS = ((0, 1), (1, 1), (2, 2), (2, 3), (0, 2), (1, 2), (0, 3), (1, 3))
                ONE_PART = tuple((k, q) for q in range(1, 4) for k in range(GROUP))
                STEPS = [TWO_PARTS if g in IN_PARTS else ONE_PART for g in range(GROUPS)]
                BEFORE = [sum(len(s) - 1 for s in STEPS[:g]) for g in range(GROUPS + 1)]

                def sample(t, g):
                    dve.wait_ge(scaled, t * GROUPS + g + 1)
                    steps = STEPS[g]
                    for i, (k, q) in enumerate(steps):
                        parts = g in IN_PARTS and k == GROUP - 1
                        if q > 1 and not parts:
                            dve.wait_ge(summed, t * BEFORE[GROUPS] + BEFORE[g] + steps.index((k, q - 1)) + 1)
                        v = val_too[:, g, :] if parts and q == 3 else val[:, g, k, :]
                        nc.vector.scalar_tensor_tensor(
                            out=v, in0=gather2[:, g * GROUP + k, q, :],
                            scalar=weight(t, g * GROUP + k, q), in1=v, op0=ALU.mult, op1=ALU.add)\
                            .then_inc(sampled if i == len(steps) - 1 else summed, 1)

                def lower(t, g):
                    dve.wait_ge(hi_ready, t * GROUPS + g + 1)
                    dve.wait_ge(multiplied, t * GROUPS + g + 1)
                    nc.vector.tensor_tensor(val_lo[:, g, :], group_t(g), val_hi[:, g, :].bitcast(f32),
                                            ALU.subtract).then_inc(lo_ready, 1)

                def relu(t):
                    dve.wait_ge(biased, t + 1 + 1)
                    nc.vector.scalar_tensor_tensor(out=z_sb, in0=z_sb, scalar=SLOPE, in1=z_sb,
                                                   op0=ALU.mult, op1=ALU.max).then_inc(activated, 1)

                def residual(t, j, quarter, c):
                    dve.wait_ge(x_loaded[quarter], (c + 1) * 32)
                    dve.wait_ge(activated, t + 1)
                    here = stage[:, :, ds(j * P, P)]
                    nc.vector.tensor_tensor(here, z_sb, here, ALU.add).then_inc(finished, 1)

                def tile(t, j_before, first=False, last=False, quarter=0, c=0):
                    for g in range(GROUPS):
                        if g == 2 and not first:
                            relu(t - 1)
                        if not last:
                            sample(*ahead(t, g, 3))
                        if not (last and g + 2 >= GROUPS):
                            lower(*ahead(t, g, 2))
                        if g == 2 and not first:
                            residual(t - 1, j_before, quarter, c)

                dve.sem_inc(sampled, GROUPS)
                dve.sem_inc(lo_ready, GROUPS)
                dve.sem_inc(finished, 1)
                for g in range(GROUPS):
                    sample(0, g)
                lower(0, 0)
                lower(0, 1)
                tile(0, 0, first=True)
                def finish_chunk(c, tiles):
                    for quarter, (j0, n) in enumerate(QUARTERS):
                        n = min(n, tiles - j0)
                        with dve.Fori(j0, j0 + n) as j:
                            tile(c * CHUNK + j + 1, j, quarter=quarter, c=c)

                with dve.Fori(0, CHUNKS - 1) as c:
                    finish_chunk(c, CHUNK)
                finish_chunk(CHUNKS - 1, CHUNK - 2)
                tile(TILES - 1, CHUNK - 2, last=True, quarter=3, c=CHUNKS - 1)
                relu(TILES - 1)
                residual(TILES - 1, CHUNK - 1, 3, CHUNKS - 1)

            @block.tensor
            def _(pe):
                def transpose(t, g):
                    pe.wait_ge(sampled, t * GROUPS + g + 1 + GROUPS)
                    pe.wait_ge(lo_ready, t * GROUPS + g + 1)
                    for k in range(GROUP):
                        for kt in range(KT2):
                            n, ch = (k * KT2 + kt) * P, slice(kt * P, (kt + 1) * P)
                            parts = [val[:, g, k, ch]] + [val_too[:, g, ch]] * (g in IN_PARTS and k == GROUP - 1)
                            for i, v in enumerate(parts):
                                last = nc.tensor.matmul(group_t(g)[:, n:n + P], v, ident[:, :],
                                                        start=(i == 0), stop=(i == len(parts) - 1),
                                                        is_transpose=True)
                    last.then_inc(transposed, 1)

                def multiply(t, g):
                    pe.wait_ge(lo_ready, t * GROUPS + g + 1 + GROUPS)
                    for s in range(GROUP * KT2):
                        slab = g * GROUP * KT2 + s
                        for a, b in ((val_hi, w2_hi), (val_hi, w2_lo), (val_lo, w2_hi)):
                            last = nc.tensor.matmul(
                                psum_acc, a[:, g, s * P:(s + 1) * P], b[:, slab, :],
                                start=(slab == 0 and b is w2_hi and a is val_hi),
                                stop=(slab == SLABS - 1 and a is val_lo))
                    last.then_inc(multiplied, 1)

                def turn(t):
                    pe.wait_ge(acc_copied, t + 1)
                    pe.wait_ge(biased, t + 1)
                    for k in range(KT1):
                        last = nc.tensor.transpose(psum_out[:, k * P:(k + 1) * P],
                                                   acc_sb[:, k * P:(k + 1) * P], ident[:, :])
                    last.then_inc(turned, 1)

                def tile(t, first=False, last=False):
                    for g in range(GROUPS):
                        if not (last and g + 2 >= GROUPS):
                            transpose(*ahead(t, g, 2))
                        if g == 0 and not first:
                            pe.wait_ge(acc_copied, t)
                        if g == 1 and not first:
                            turn(t - 1)
                        multiply(t, g)

                pe.sem_inc(transposed, GROUPS)
                pe.sem_inc(multiplied, GROUPS)
                pe.sem_inc(turned, 1)
                transpose(0, 0)
                transpose(0, 1)
                tile(0, first=True)
                with pe.Fori(1, TILES - 1) as t:
                    tile(t)
                tile(TILES - 1, last=True)
                turn(TILES - 1)


PLAN_STEPS_1 = 12
PLAN_STEPS_2 = 13


def kernel(**inputs):
    import concourse.bacc as bacc
    from concourse.bass_utils import run_bass_kernel_spmd as run

    a = {k.removeprefix("L0_conv_"): np.asarray(v) for k, v in inputs.items()}
    where, inside, shift = pixel_constants()
    arrays = {
        "x": a["x"].reshape(N_IMAGES, C_OUT, IMAGE),
        "w1": np.pad(np.concatenate([a["w1"][:, :, 0, 0], a["w_off1"][:, :, 0, 0]]), ((0, 1), (0, 0))).T,
        "norm1": np.stack([a[n] for n in ("g1", "v1", "m1", "bb1", "b1")]),
        "w_off2": np.pad(a["w_off2"].transpose(2, 1, 3, 0), ((0, 0), (0, 0), (0, 0), (0, DX - 3 * TAPS)))
        .reshape(3, C_MID, 3 * DX),
        "w2": a["w2"].transpose(2, 3, 1, 0).reshape(TAPS * C_MID, C_OUT),
        "norm2": np.stack([a[n] for n in ("g2", "v2", "m2", "bb2", "b2")]),
        "norm2_col": np.stack([a[n] for n in ("g2", "v2", "m2", "bb2", "b2")])
        .reshape(5, C_OUT // P, P).transpose(2, 0, 1),
        "b_off1": a["b_off1"].reshape(1, 3),
        "b_off2": a["b_off2"].reshape(1, 3 * TAPS),
        "where": where,
        "inside": inside,
        "shift": shift,
        "identity": np.eye(P, dtype=np.float32),
    }
    arrays = {k: np.ascontiguousarray(v) for k, v in arrays.items()}
    nc = bacc.Bacc("TRN2", target_bir_lowering=False, num_devices=1)
    args = [nc.dram_tensor(k, v.shape, mybir.dt.from_np(v.dtype), kind="ExternalInput").ap()
            for k, v in arrays.items()]
    out = nc.dram_tensor("out", (N_IMAGES, C_OUT, IMAGE), mybir.dt.float32, kind="ExternalOutput").ap()
    deformable_kernel(nc, *args, out)
    r = run(nc, [arrays], core_ids=[0])
    return r.results[0]["out"].reshape(N_IMAGES, C_OUT, HEIGHT, WIDTH)
```
